# Optimizing a Trainium2 kernel written in Bass

```python
import numpy as np
import jax
import jax.numpy as jnp

def _softmax(x, axis=-1):
    return jax.nn.softmax(x, axis=axis)

def _gelu(x):
    return jax.nn.gelu(x, approximate=True)

def _silu(x):
    return jax.nn.silu(x)

def _sigmoid(x):
    return jax.nn.sigmoid(x)

def _layernorm(x, axis=-1, eps=1e-05):
    m = jnp.mean(x, axis=axis, keepdims=True)
    v = jnp.var(x, axis=axis, keepdims=True)
    return (x - m) / jnp.sqrt(v + eps)

def _scatter_add(tgt, idx, src, axis=0):
    return tgt.at[idx].add(src)

def _segment_sum(src, seg, n):
    return jax.ops.segment_sum(src, seg, n)
kernel_name = 'mk_seq_preln_d1_jaxref_r8_dd3721'

def setup_inputs(seed: int=0):
    np.random.seed(seed)
    _w = jnp.asarray

    def _L0_attn_setup():
        import jax, jax.numpy as jnp
        import numpy as np
        B, L, D_IN, D_OUT, H, WIN = (1, 256, 128, 128, 16, 64)
        D_H = D_OUT // H
        key = jax.random.key(seed)
        ks = jax.random.split(key, 5)
        s = 0.02
        return {'x': jax.random.normal(ks[0], (B, L, D_IN), dtype=jnp.float32), 'Wq': jax.random.normal(ks[1], (D_IN, D_OUT), dtype=jnp.float32) * s, 'Wk': jax.random.normal(ks[2], (D_IN, D_OUT), dtype=jnp.float32) * s, 'Wv': jax.random.normal(ks[3], (D_IN, D_OUT), dtype=jnp.float32) * s, 'Wo': jax.random.normal(ks[4], (D_OUT, D_IN), dtype=jnp.float32) * s}
    _L0_attn_in = _L0_attn_setup()

    def _L0_ffn_setup():
        import jax, jax.numpy as jnp
        import numpy as np
        TOP_K = 2
        CAPACITY_FACTOR = 1.0
        key = jax.random.key(seed)
        ks = jax.random.split(key, 4)
        sl, bs, hs, ffn, E = (256, 8, 128, 512, 8)
        x = jax.random.normal(ks[0], (sl, bs, hs), dtype=jnp.float32)
        w_router = jax.random.normal(ks[1], (hs, E), dtype=jnp.float32) * 0.02
        w1 = jax.random.normal(ks[2], (E, hs, ffn), dtype=jnp.float32) * 0.02
        w2 = jax.random.normal(ks[3], (E, ffn, hs), dtype=jnp.float32) * 0.02
        bias = jnp.zeros((1, 1, hs), dtype=jnp.float32)
        return {'x': x, 'w_router': w_router, 'w1': w1, 'w2': w2, 'bias': bias}
    _L0_ffn_in = _L0_ffn_setup()
    _d = {'L0_attn_x': _L0_attn_in['x'], 'L0_attn_Wq': _L0_attn_in['Wq'], 'L0_attn_Wk': _L0_attn_in['Wk'], 'L0_attn_Wv': _L0_attn_in['Wv'], 'L0_attn_Wo': _L0_attn_in['Wo'], 'L0_ffn_w_router': _L0_ffn_in['w_router'], 'L0_ffn_w1': _L0_ffn_in['w1'], 'L0_ffn_w2': _L0_ffn_in['w2'], 'L0_ffn_bias': _L0_ffn_in['bias']}
    _x0 = _d['L0_attn_x']
    _d['L0_attn_x'] = jax.random.normal(jax.random.fold_in(jax.random.key(seed), 1), (8, 1024, 128), dtype=_x0.dtype)
    del _x0
    return _d

def reference(L0_attn_x, L0_attn_Wq, L0_attn_Wk, L0_attn_Wv, L0_attn_Wo, L0_ffn_w_router, L0_ffn_w1, L0_ffn_w2, L0_ffn_bias):

    def _L0_attn_ref(x, Wq, Wk, Wv, Wo):
        import jax, jax.numpy as jnp
        import numpy as np
        B, L, D_IN, D_OUT, H, WIN = (1, 256, 128, 128, 16, 64)
        D_H = D_OUT // H
        Bx, Lx, _ = x.shape
        W = min(WIN, Lx)
        scale = D_H ** (-0.5)

        def split_heads(t):
            return t.reshape(Bx, Lx, H, D_H).transpose(0, 2, 1, 3)
        q = split_heads(x @ Wq)
        k = split_heads(x @ Wk)
        v = split_heads(x @ Wv)
        offsets = jnp.arange(W) - (W - 1)
        idx = jnp.arange(Lx)[:, None] + offsets[None, :]
        invalid = idx < 0
        idx = jnp.clip(idx, 0, Lx - 1)
        k_win = jnp.take(k, idx, axis=2)
        v_win = jnp.take(v, idx, axis=2)
        scores = jnp.einsum('bhld,bhlwd->bhlw', q, k_win) * scale
        scores = jnp.where(invalid[None, None, :, :], -jnp.inf, scores)
        attn = jax.nn.softmax(scores, axis=-1)
        ctx = jnp.einsum('bhlw,bhlwd->bhld', attn, v_win)
        ctx = ctx.transpose(0, 2, 1, 3).reshape(Bx, Lx, D_OUT)
        return ctx @ Wo

    def _L0_ffn_ref(x, w_router, w1, w2, bias):
        import jax, jax.numpy as jnp
        import numpy as np
        TOP_K = 2
        CAPACITY_FACTOR = 1.0
        sl, bs, hs = x.shape
        E = w_router.shape[1]
        xf = x.reshape(-1, hs)
        T = xf.shape[0]
        capacity = int(CAPACITY_FACTOR * TOP_K * T / E)
        scores = jax.nn.softmax(xf @ w_router, axis=-1)
        expert_weights, top_experts = jax.lax.top_k(scores, TOP_K)
        flat_e = top_experts.reshape(-1)
        flat_w = expert_weights.reshape(-1)
        N = flat_e.shape[0]
        order = jnp.argsort(flat_e, stable=True)
        bin_ids = flat_e[order]
        tpe = jnp.zeros((E,), jnp.int32).at[flat_e].add(1)
        starts = jnp.cumsum(tpe) - tpe
        offsets = jnp.arange(N) - starts[bin_ids]
        valid = offsets < capacity
        slot = jnp.where(valid, bin_ids * capacity + offsets, E * capacity)
        src = order // TOP_K
        xb = jnp.zeros((E * capacity + 1, hs), x.dtype).at[slot].set(xf[src])
        xb = xb[:-1].reshape(E, capacity, hs)
        h = jax.nn.gelu(jnp.einsum('ech,ehf->ecf', xb, w1))
        y = jnp.einsum('ecf,efh->ech', h, w2).reshape(E * capacity, hs)
        yv = jnp.where(valid[:, None], y[jnp.minimum(slot, E * capacity - 1)], 0.0)
        out = jnp.zeros((T, hs), x.dtype).at[src].add(flat_w[order][:, None] * yv)
        return out.reshape(sl, bs, hs) + bias
    x = L0_attn_x
    x = x + _L0_attn_ref(_layernorm(x, axis=-1), L0_attn_Wq, L0_attn_Wk, L0_attn_Wv, L0_attn_Wo)
    x = x + _L0_ffn_ref(_layernorm(x, axis=-1), L0_ffn_w_router, L0_ffn_w1, L0_ffn_w2, L0_ffn_bias)
    return x

_drawn_inputs = setup_inputs


def setup_inputs(seed=0):
    import zlib

    import numpy as np

    out = dict(_drawn_inputs(seed))
    spreads = {'L0_ffn_bias': (0.0, 0.1)}
    factors = {'L0_attn_Wq': 8.0,
     'L0_attn_Wk': 8.0,
     'L0_attn_Wv': 8.0,
     'L0_attn_Wo': 7.971,
     'L0_ffn_w_router': 5.303,
     'L0_ffn_w1': 4.756,
     'L0_ffn_w2': 4.689}
    for name, (base, spread) in spreads.items():
        noise = np.random.default_rng([zlib.crc32(name.encode()), seed]).standard_normal(out[name].shape)
        drawn = base * np.exp(spread * noise) if base else spread * noise
        out[name] = jnp.asarray(drawn.astype(out[name].dtype))
    for name, factor in factors.items():
        out[name] = (out[name] * factor).astype(out[name].dtype)
    return out
```

```python
import concourse.bass as bass
from concourse import mybir
from contextlib import ExitStack

F32 = mybir.dt.float32
BF16 = mybir.dt.bfloat16
I32 = mybir.dt.int32
U32 = mybir.dt.uint32
ALU = mybir.AluOpType
ACT = mybir.ActivationFunctionType
AX = mybir.AxisListType

BATCH, SEQ, D = 8, 1024, 128
H, DH, WIN = 16, 8, 64
E, TOPK, F = 8, 2, 512
T = BATCH * SEQ
CAP = TOPK * T // E
P = 128
NTILE = T // P
NPAIR = NTILE // 2
PAIRS_PER_SEQ = SEQ // (2 * P)
GROUP = SEQ // P
NGROUP = NTILE // GROUP
BLK = WIN
UNITS = 8
HP = H // 2
VW = 2 * DH + 2
ROW = D + E + 1
SPP = CAP // P
NEG = -1.0e30
EPS = 1e-5
MAGIC = float(0x5F3759DF)
LOWEST = -104.0
FC = F // P
CHUNKS = SPP // 4
ADDED = 16 * 4 * CHUNKS // 2


def moe_block_kernel(nc, x, wq, wk, wv, wo, w_router, w1, w2, bias, out):
    ctx = ExitStack()
    with ctx:
        def sb(name, shape, dt=F32):
            return ctx.enter_context(nc.sbuf_tensor(name, shape, dt))

        def sem(name):
            return ctx.enter_context(nc.semaphore(name))

        slots_dram = nc.dram_tensor("slots_dram", (E * CAP, ROW), F32, kind="Internal").ap()

        x_sb = sb("x_sb", [P, 2 * (NPAIR + 3), D])
        rows_sb = sb("rows_sb", [P, 2 * (NPAIR + 1), ROW])
        logits_sb = sb("logits_sb", [P, 2 * (NPAIR + 1), E])
        wq_sb = sb("wq_sb", [P, D])
        wk_sb = sb("wk_sb", [P, D])
        wv_sb = sb("wv_sb", [P, D])
        wo_sb = sb("wo_sb", [HP * DH, 2, D])
        wr_sb = sb("wr_sb", [P, E])
        bias_sb = sb("bias_sb", [P, D])
        ident = sb("ident", [P, P])
        headmask = sb("headmask", [P, H])
        blocksel = sb("blocksel", [BLK, P], BF16)
        window = sb("window", [BLK, PAIRS_PER_SEQ, 2, P], BF16)
        before = sb("before", [P, P], BF16)
        ones = sb("ones", [P, P], BF16)
        erank = sb("erank", [P, E])
        eslot = sb("eslot", [P, E])
        empty_rows = sb("empty_rows", [P, SPP, ROW])
        stats = sb("stats", [P, 4, 6])
        meanvar = sb("meanvar", [P, 4, 2])
        veps = sb("veps", [P, 4])
        rs_i = sb("rs_i", [P, 4], I32)
        rs_a = sb("rs_a", [P, 4])
        rs_y = sb("rs_y", [P, 4])
        xn = sb("xn", [P, 2, D])
        xn2 = sb("xn2", [P, 2, D])
        xn2T = sb("xn2T", [P, 2 * P])
        xnT = sb("xnT", [P, BLK + 2 * P])
        qT = sb("qT", [P, 2, 2 * P])
        kT = sb("kT", [P, 2, BLK + 2 * P])
        v_sb = sb("v_sb", [P, 2, 4, HP, VW])
        qbd = [sb(f"qbd{s}", [P, 2, H, BLK]) for s in range(2)]
        negmax = sb("negmax", [P, 4, 4])
        probs = sb("probs", [P, 2, 4, P])
        probsT = sb("probsT", [P, 2, 4, P])
        rden = sb("rden", [P, 2, 2 * HP])
        ctx_sb = sb("ctx_sb", [P, 2, 3 * HP, DH])
        ctxT = sb("ctxT", [HP * DH, 2, 2, 2, BLK])
        xbias = sb("xbias", [P, 2, 2, D])
        r_m = sb("r_m", [P, GROUP])
        r_sh = sb("r_sh", [P, GROUP, E])
        r_ex = sb("r_ex", [P, GROUP, E])
        r_t = sb("r_t", [P, GROUP, E])
        r_oh = sb("r_oh", [P, 2, GROUP, E])
        r_sel = sb("r_sel", [P, GROUP + 1, E], BF16)
        r_pos = sb("r_pos", [P, GROUP, E])
        r_cnt = sb("r_cnt", [P, E])
        send_rows = sb("send_rows", [P, GROUP, ROW])
        slot_id = sb("slot_id", [P, 2, GROUP], I32)
        w1_sb = sb("w1_sb", [P, 2, F])
        w2_sb = sb("w2_sb", [P, 2, FC, D])
        xg = sb("xg", [P, 2, SPP, ROW])
        xgT = sb("xgT", [P, 2, 4 * P])
        hT = sb("hT", [P, 2, FC, 4 * P])
        y_sb = sb("y_sb", [P, 2, 4, D])

        bank = [ctx.enter_context(nc.psum_tensor(f"bank{i}", [P, 512], F32)) for i in range(8)]
        scores = bank[0:4]
        pt_ps = bank[4]
        o_ps = bank[5:7]
        misc = bank[7]
        CTX_T, ATT = 0, 256

        def ctx_view(s):
            return o_ps[s][:, 0:2 * HP * VW].rearrange("p (j c) -> p j c", c=VW)

        ld_w = sem("ld_w")
        ld_x = [sem(f"ld_x{i}") for i in range(2)]
        c_pool = sem("c_pool")
        c_dve = sem("c_dve")
        dve_chain = sem("dve_chain")
        d_init = sem("d_init")
        s_xn = sem("s_xn")
        s_xn2 = sem("s_xn2")
        s_xnT = sem("s_xnT")
        s_xnT_sb = sem("s_xnT_sb")
        s_qk = sem("s_qk")
        s_qk_sb = sem("s_qk_sb")
        s_v = sem("s_v")
        s_v_sb = sem("s_v_sb")
        s_qbd = sem("s_qbd")
        s_scores = sem("s_scores")
        s_max = sem("s_max")
        s_exp = sem("s_exp")
        s_pt = sem("s_pt")
        s_pt_sb = sem("s_pt_sb")
        s_pv = sem("s_pv")
        s_ctx = sem("s_ctx")
        s_ctxT = sem("s_ctxT")
        s_ctxT_sb = sem("s_ctxT_sb")
        s_att = sem("s_att")
        s_x2 = sem("s_x2")
        s_xn2T = sem("s_xn2T")
        s_xn2T_sb = sem("s_xn2T_sb")
        s_lg = sem("s_lg")
        s_lg_sb = sem("s_lg_sb")
        s_rows = sem("s_rows")
        s_xbias = sem("s_xbias")
        s_out = sem("s_out")
        s_shift = sem("s_shift")
        s_rexp = sem("s_rexp")
        s_sel = sem("s_sel")
        s_pos = sem("s_pos")
        s_slot = sem("s_slot")
        s_send = sem("s_send")
        s_turn_sp = sem("s_turn_sp")
        s_turn_pool = sem("s_turn_pool")
        s_scat = sem("s_scat")
        ld_e = [sem(f"ld_e{i}") for i in range(2)]
        ld_g = [sem(f"ld_g{i}") for i in range(2)]
        f_xT = sem("f_xT")
        f_xT_sb = sem("f_xT_sb")
        f_h = sem("f_h")
        f_gelu = sem("f_gelu")
        f_y = sem("f_y")
        f_y_sb = sem("f_y_sb")
        f_add = [sem(f"f_add{i}") for i in range(2)]

        block = ctx.enter_context(nc.Block())
        N_POOL_CONST = 0

        @block.sync
        def _(sp):
            xr = x.rearrange("b (s p) d -> p (b s) d", p=P)
            sp.dma_start(x_sb[:, 2:2 + 16, :], xr[:, 0:16, :]).then_inc(ld_x[0], 16)
            for src, dst in ((wq, wq_sb), (wk, wk_sb), (wv, wv_sb), (w_router, wr_sb)):
                sp.dma_start(dst[:, :], src).then_inc(ld_w, 16)
            wo4 = wo.rearrange("(j two d) n -> two j d n", two=2, d=DH)
            for two in range(2):
                for j in range(HP):
                    sp.dma_start(wo_sb[j * DH:(j + 1) * DH, two, :], wo4[two, j]).then_inc(ld_w, 16)
            sp.dma_start(bias_sb[:, :], bias.rearrange("a b d -> (a b) d").to_broadcast([P, D])).then_inc(ld_w, 16)
            sp.dma_start(x_sb[:, 18:2 + NTILE, :], xr[:, 16:NTILE, :]).then_inc(ld_x[1], 16)
            sp.wait_ge(c_pool, 2)
            for e in range(E):
                sp.dma_start(slots_dram[e * CAP:(e + 1) * CAP, :].rearrange("(p j) w -> p (j w)", p=P),
                             empty_rows[:, :, :].rearrange("p j w -> p (j w)")).then_inc(d_init, 16)
            sp.dma_start(out[T:T + CAP, :].rearrange("(p j) w -> p j w", p=P),
                         empty_rows[:, :, 0:D]).then_inc(d_init, 16)
            out_tiles = out[0:T, :].rearrange("(t p) d -> p t d", p=P)
            with sp.Fori(0, NPAIR) as n:
                sp.wait_ge(s_xbias, n + 1)
                sp.dma_start(out_tiles[:, bass.ds(2 * n, 2), :],
                             xbias[:, bass.ds(n % 2, 1)].rearrange("p o s d -> p (o s) d")).then_inc(s_out, 16)
                sp.wait_ge(s_out, 16 * n + 16)
                sp.sem_inc(s_turn_sp, 1)
            slots_e = slots_dram.rearrange("(e p j) w -> p e (j w)", e=E, p=P)
            w1_e = w1.rearrange("e h f -> h e f")
            w2_e = w2.rearrange("e (c p) h -> p e c h", p=P)
            sp.wait_ge(s_out, 16 * NPAIR)
            sp.wait_ge(d_init, 16 * (E + 1))
            sp.wait_ge(s_scat, 16 * TOPK * NTILE)

            def load_expert(e, r):
                sp.dma_start(w1_sb[:, r:r + 1, :], w1_e[:, bass.ds(e, 1), :]).then_inc(ld_e[r], 16)
                sp.dma_start(w2_sb[:, r:r + 1, :, :], w2_e[:, bass.ds(e, 1)]).then_inc(ld_e[r], 16)
                sp.dma_start(xg[:, r:r + 1, :, :].rearrange("p o j w -> p o (j w)"),
                             slots_e[:, bass.ds(e, 1), :]).then_inc(ld_g[r], 16)

            load_expert(0, 0)
            load_expert(1, 1)
            with sp.Fori(1, E // 2) as ee:
                for r in range(2):
                    for i in range(2):
                        sp.wait_ge(f_add[i], ADDED * (2 * ee - 1 + r))
                        sp.sem_inc(s_turn_sp, 1)
                    load_expert(2 * ee + r, r)

        @block.gpsimd
        def _(pool):
            pool.memset(empty_rows[:, :, :], 0.0).then_inc(c_pool, 1)
            pool.wait_ge(c_pool, 1)
            pool.iota(empty_rows[:, :, ROW - 1].bitcast(I32), pattern=[[1, SPP]], base=T,
                      channel_multiplier=SPP).then_inc(c_pool, 1)
            pool.memset(ident[:, :], 0.0).then_inc(c_pool, 1)
            pool.memset(blocksel[:, :], 0.0).then_inc(c_pool, 1)
            pool.memset(window[:, :, :, :], 0.0).then_inc(c_pool, 1)
            pool.memset(before[:, :], 1.0).then_inc(c_pool, 1)
            pool.memset(headmask[:, :], 1.0).then_inc(c_pool, 1)
            pool.iota(rows_sb[:, 2:2 + NTILE, ROW - 1].bitcast(I32), pattern=[[P, NTILE]], base=0,
                      channel_multiplier=1).then_inc(c_pool, 1)
            pool.iota(erank[:, :], pattern=[[-1, E]], base=E, channel_multiplier=0,
                      allow_small_or_imprecise_dtypes=True).then_inc(c_pool, 1)
            pool.iota(eslot[:, :], pattern=[[CAP, E]], base=0, channel_multiplier=0,
                      allow_small_or_imprecise_dtypes=True).then_inc(c_pool, 1)
            pool.wait_ge(c_pool, 10)
            pool.affine_select(out=ident[:, :], in_=ident[:, :], compare_op=ALU.not_equal, fill=1.0, base=0,
                               pattern=[[-1, P]], channel_multiplier=1).then_inc(c_pool, 1)
            pool.affine_select(out=blocksel[:, :], in_=blocksel[:, :], compare_op=ALU.not_equal, fill=1.0,
                               base=0, pattern=[[0, 2], [-1, BLK]], channel_multiplier=1).then_inc(c_pool, 1)
            pool.affine_select(out=window[:, :, :, :], in_=window[:, :, :, :], compare_op=ALU.is_gt, fill=NEG,
                               base=0, pattern=[[0, PAIRS_PER_SEQ], [0, 2], [1, P]],
                               channel_multiplier=-1).then_inc(c_pool, 1)
            pool.affine_select(out=before[:, :], in_=before[:, :], compare_op=ALU.is_gt, fill=0.0, base=0,
                               pattern=[[1, P]], channel_multiplier=-1).then_inc(c_pool, 1)
            pool.affine_select(out=headmask[:, :], in_=headmask[:, :], compare_op=ALU.is_ge, fill=0.0, base=0,
                               pattern=[[-DH, H]], channel_multiplier=1).then_inc(c_pool, 1)
            pool.wait_ge(c_pool, 15)
            pool.affine_select(out=window[:, :, :, :], in_=window[:, :, :, :], compare_op=ALU.is_ge, fill=NEG,
                               base=WIN, pattern=[[0, PAIRS_PER_SEQ], [0, 2], [-1, P]],
                               channel_multiplier=1).then_inc(c_pool, 1)
            pool.affine_select(out=headmask[:, :], in_=headmask[:, :], compare_op=ALU.is_ge, fill=0.0,
                               base=DH - 1, pattern=[[DH, H]], channel_multiplier=-1).then_inc(c_pool, 1)
            pool.wait_ge(c_pool, 17)
            pool.memset(window[:, 0, 0, 0:BLK], NEG).then_inc(c_pool, 1)

            def spread_queries(m, s):
                q = qT[:, bass.ds(m % 2, 1), s * P:(s + 1) * P].rearrange("p o (b q) -> p (o b) q", b=2)
                pool.tensor_tensor(out=qbd[s][:, :, :, :],
                                   in0=q.unsqueeze(2).to_broadcast([P, 2, H, BLK]),
                                   in1=headmask[:, :].unsqueeze(1).unsqueeze(3).to_broadcast([P, 2, H, BLK]),
                                   op=ALU.mult).then_inc(s_qbd, 1)

            def keep_rows(n):
                pool.wait_ge(s_xn2, n + 1)
                pool.tensor_copy(rows_sb[:, bass.ds(2 * n, 2), 0:D], xn2[:, :, :]).then_inc(s_rows, 1)

            pool.wait_ge(s_qk_sb, 1)
            spread_queries(0, 0)
            spread_queries(0, 1)
            pool.wait_ge(ld_w, 16 * 21)
            with pool.Fori(0, NPAIR) as n:
                pool.wait_ge(s_qk_sb, n + 2)
                pool.wait_ge(s_scores, UNITS * n + 4)
                spread_queries(n + 1, 0)
                keep_rows(n)
                pool.wait_ge(s_scores, UNITS * n + 8)
                spread_queries(n + 1, 1)
                pool.wait_ge(s_x2, 2 * n + 2)
                pool.wait_ge(s_out, 16 * n)
                pool.tensor_tensor(out=xbias[:, bass.ds(n % 2, 1)].rearrange("p o s d -> p (o s) d"),
                                   in0=x_sb[:, bass.ds(2 * n + 2, 2), :],
                                   in1=bias_sb[:, :].unsqueeze(1).to_broadcast([P, 2, D]),
                                   op=ALU.add).then_inc(s_xbias, 1)
            keep_rows(NPAIR)

            pool.wait_ge(s_rows, NPAIR + 1)
            with pool.Fori(0, NGROUP) as g:
                pool.wait_ge(s_slot, g + 1)
                pool.wait_ge(s_scat, 16 * TOPK * GROUP * g)
                pool.tensor_copy(send_rows[:, :, :], rows_sb[:, bass.ds(2 + g * GROUP, GROUP), :]).then_inc(s_send, 1)
                pool.wait_ge(s_send, g + 1)
                pool.sem_inc(s_turn_pool, 1)
                pool.wait_ge(d_init, 16 * (E + 1))
                for j in range(GROUP):
                    for k in range(2):
                        pool.indirect_dma_start(
                            out=slots_dram,
                            out_offset=bass.IndirectOffsetOnAxis(ap=slot_id[:, k, j:j + 1].bitcast(U32), axis=0),
                            in_=send_rows[:, j, :],
                            in_offset=None, bounds_check=E * CAP - 1, oob_is_err=False).then_inc(s_scat, 16)

            def add_results(ee, r):
                for c in range(CHUNKS):
                    pool.wait_ge(f_y_sb, (2 * ee + r) * CHUNKS + c + 1)
                    pool.sem_inc(s_turn_pool, 1)
                    pool.wait_ge(d_init, 16 * (E + 1))
                    for k in range(4):
                        pool.indirect_dma_start(
                            out=out,
                            out_offset=bass.IndirectOffsetOnAxis(
                                ap=xg[:, r, 4 * c + k, ROW - 1:ROW].bitcast(U32), axis=0),
                            in_=y_sb[:, c % 2, k, :],
                            in_offset=None, bounds_check=T + CAP - 1, oob_is_err=True,
                            compute_op=ALU.add).then_inc(f_add[c % 2], 16)
                for i in range(2):
                    pool.wait_ge(f_add[i], ADDED * (2 * ee + r + 1))
                    pool.sem_inc(s_turn_pool, 1)

            pool.wait_ge(s_out, 16 * NPAIR)
            with pool.Fori(0, E // 2) as ee:
                for r in range(2):
                    add_results(ee, r)

        @block.scalar
        def _(act):
            def query_key(m):
                act.wait_ge(s_qk, m + 1)
                nc.scalar.activation(qT[:, bass.ds(m % 2, 1), :].rearrange("p o q -> p (o q)"),
                                     misc[:, 0:2 * P], ACT.Copy, scale=float(DH) ** -0.5)
                nc.scalar.activation(kT[:, bass.ds(m % 2, 1), BLK:].rearrange("p o q -> p (o q)"),
                                     misc[:, 2 * P:4 * P], ACT.Copy).then_inc(s_qk_sb, 1)

            def query_key_next(n):
                act.wait_ge(s_qk_sb, n + 1)
                nc.scalar.activation(kT[:, bass.ds((n + 1) % 2, 1), 0:BLK].rearrange("p o q -> p (o q)"),
                                     kT[:, bass.ds(n % 2, 1), 2 * P:].rearrange("p o q -> p (o q)"), ACT.Copy)
                query_key(n + 1)

            def exps(n, k):
                act.wait_ge(s_max, UNITS * n + k + 1)
                for c in range(4):
                    last = nc.scalar.activation(probs[:, k % 2, c, :], scores[k % 4][:, c * P:(c + 1) * P], ACT.Exp,
                                                bias=negmax[:, k % 4, c:c + 1])
                last.then_inc(s_exp, 1)

            def context_T(n, s):
                act.wait_ge(s_ctxT, 2 * n + s + 1)
                nc.scalar.activation(ctxT[:, s, :, :, :],
                                     o_ps[s][0:HP * DH, CTX_T:CTX_T + 2 * P].rearrange(
                                         "p (b h q) -> p h b q", b=2, h=2), ACT.Copy).then_inc(s_ctxT_sb, 1)

            def router_T(n):
                act.wait_ge(s_xn2T, n + 1)
                nc.scalar.activation(xn2T[:, :], misc[:, 0:2 * P], ACT.Copy).then_inc(s_xn2T_sb, 1)

            act.wait_ge(c_dve, 1)
            query_key(0)
            with act.Fori(0, NPAIR) as n:
                for k in range(UNITS):
                    exps(n, k)
                    if k == 2:
                        query_key_next(n)
                    if k == 6:
                        context_T(n, 0)
                router_T(n)
                context_T(n, 1)
            router_T(NPAIR)

            with act.Fori(0, NGROUP) as g:
                act.wait_ge(s_shift, g + 1)
                nc.scalar.activation(r_ex[:, :, :], r_sh[:, :, :], ACT.Exp).then_inc(s_rexp, 1)

            with act.Fori(0, E // 2) as ee:
                for c in range(2 * CHUNKS):
                    for f in range(FC):
                        act.wait_ge(f_h, (ee * 2 * CHUNKS + c) * FC + f + 1)
                        nc.scalar.activation(hT[:, c % 2, f, :], bank[f][:, :], ACT.Gelu_apprx_tanh).then_inc(f_gelu, 1)

        @block.vector
        def _(dve):
            class Chain:
                def __init__(self, base):
                    self.base, self.steps = base, 0

                def then(self, instruction):
                    instruction.then_inc(dve_chain, 1)
                    self.steps += 1
                    dve.wait_ge(dve_chain, self.base + self.steps)

            def norms(chain, first, second, m):
                tiles = [x_sb[:, bass.ds(2 * a + 2 + s, 1), :].rearrange("p o d -> p (o d)")
                         for a in (first, second) if a is not None for s in range(2)]
                w = len(tiles)
                for i, t in enumerate(tiles):
                    last = nc.vector.bn_stats(stats[:, i, :], t)
                chain.then(last)
                v, y, a = veps[:, 0:w], rs_y[:, 0:w], rs_a[:, 0:w]
                mean, diff = meanvar[:, 0:w, 0], meanvar[:, 0:w, 1]
                nc.vector.tensor_tensor(out=mean, in0=stats[:, 0:w, 1], in1=stats[:, 0:w, 4], op=ALU.add)
                nc.vector.tensor_tensor(out=v, in0=stats[:, 0:w, 2], in1=stats[:, 0:w, 5], op=ALU.add)
                chain.then(nc.vector.tensor_tensor(out=diff, in0=stats[:, 0:w, 1], in1=stats[:, 0:w, 4], op=ALU.subtract))
                nc.vector.tensor_scalar(mean, mean, 0.5, None, ALU.mult)
                nc.vector.tensor_scalar(v, v, 1.0 / D, EPS, ALU.mult, ALU.add)
                chain.then(nc.vector.scalar_tensor_tensor(out=diff, in0=diff, scalar=0.25, in1=diff, op0=ALU.mult, op1=ALU.mult))
                chain.then(nc.vector.tensor_tensor(out=v, in0=v, in1=diff, op=ALU.add))
                chain.then(nc.vector.tensor_scalar(rs_i[:, 0:w], v.bitcast(I32), 1, None, ALU.logical_shift_right))
                chain.then(nc.vector.tensor_scalar(y.bitcast(I32), rs_i[:, 0:w], -1.0, MAGIC, ALU.mult, ALU.add))
                for _ in range(3):
                    chain.then(nc.vector.scalar_tensor_tensor(out=a, in0=y, scalar=-0.5, in1=y, op0=ALU.mult, op1=ALU.mult))
                    chain.then(nc.vector.tensor_tensor(out=a, in0=a, in1=v, op=ALU.mult))
                    chain.then(nc.vector.scalar_tensor_tensor(out=y, in0=a, scalar=1.5, in1=y, op0=ALU.add, op1=ALU.mult))
                i = 0
                if first is not None:
                    for s in range(2):
                        last = nc.vector.tensor_scalar(xn[:, s, :], tiles[i], meanvar[:, i, 0:1], rs_y[:, i:i + 1],
                                                       ALU.subtract, ALU.mult)
                        i += 1
                    last.then_inc(s_xn, 1)
                if second is not None:
                    for s in range(2):
                        last = nc.vector.tensor_scalar(xn2[:, s, :], tiles[i], meanvar[:, i, 0:1], rs_y[:, i:i + 1],
                                                       ALU.subtract, ALU.mult)
                        i += 1
                    last.then_inc(s_xn2, 1)

            NORM_STEPS = 6 + 9

            def prep_T(chain, m, pull):
                dve.wait_ge(s_xnT, m + 1)
                if pull:
                    dve.wait_ge(s_xnT_sb, m)
                    chain.then(nc.vector.tensor_copy(xnT[:, 0:BLK], xnT[:, 2 * P:]))
                nc.vector.tensor_copy(xnT[:, BLK:], misc[:, 0:2 * P]).then_inc(s_xnT_sb, 1)

            def values(m):
                dve.wait_ge(s_v, m + 1)
                nc.vector.tensor_copy(v_sb[:, bass.ds(m % 2, 1), :, :, 0:2 * DH].rearrange("p o w j c -> p (o w) j c"),
                                      misc[:, :].rearrange("p (w j c) -> p w j c", w=4, j=HP)).then_inc(s_v_sb, 1)

            def score_max(n, k):
                dve.wait_ge(s_scores, UNITS * n + k + 1)
                nc.vector.tensor_reduce(negmax[:, k % 4, :], scores[k % 4][:, :].rearrange("p (c j) -> p c j", c=4),
                                        AX.X, ALU.max, negate=True).then_inc(s_max, 1)

            def probs_T(n, k):
                dve.wait_ge(s_pt, UNITS * n + k + 1)
                nc.vector.tensor_copy(probsT[:, k % 2, :, :].rearrange("p c j -> p (c j)"),
                                      pt_ps[:, :]).then_inc(s_pt_sb, 1)

            def normalise(chain, n, s):
                dve.wait_ge(s_pv, UNITS * n + 4 * s + 4)
                o = ctx_view(s)
                chain.then(nc.vector.reciprocal(rden[:, s, :], o[:, :, 2 * DH]))
                for par in range(2):
                    q = slice(par * BLK, (par + 1) * BLK)
                    last = nc.vector.tensor_tensor(out=ctx_sb[q, s, 0:2 * HP, :], in0=o[q, :, par * DH:(par + 1) * DH],
                                                   in1=rden[q, s, :].unsqueeze(2).to_broadcast([BLK, 2 * HP, DH]),
                                                   op=ALU.mult)
                last.then_inc(s_ctx, 1)

            def residual(n, s):
                dve.wait_ge(s_att, 2 * n + s + 1)
                t = x_sb[:, bass.ds(2 * n + 2 + s, 1), :].rearrange("p o d -> p (o d)")
                nc.vector.tensor_tensor(out=t, in0=o_ps[s][:, ATT:ATT + D], in1=t, op=ALU.add).then_inc(s_x2, 1)

            def logits(n):
                dve.wait_ge(s_lg, n + 1)
                nc.vector.tensor_copy(logits_sb[:, bass.ds(2 * n, 2), :].rearrange("p t e -> p (t e)"),
                                      misc[:, 0:2 * E]).then_inc(s_lg_sb, 1)

            nc.vector.memset(x_sb[:, 0:2, :], 0.0)
            nc.vector.memset(x_sb[:, 2 + NTILE:, :], 0.0)
            nc.vector.memset(kT[:, :, 0:BLK], 0.0)
            nc.vector.memset(xnT[:, 0:BLK], 0.0)
            nc.vector.memset(ones[:, :], 1.0)
            nc.vector.memset(ctx_sb[:, :, 2 * HP:, :], 0.0)
            nc.vector.memset(v_sb[:, :, :, :, 2 * DH:], 1.0)
            nc.vector.memset(r_sel[:, GROUP, :], 0.0)
            nc.vector.memset(r_cnt[:, :], 0.0).then_inc(c_dve, 1)
            dve.wait_ge(c_dve, 1)

            chain = Chain(0)
            dve.wait_ge(ld_x[0], 16)
            norms(chain, 0, None, 0)
            prep_T(chain, 0, False)
            norms(chain, 1, None, 0)
            values(0)
            score_max(0, 0)
            score_max(0, 1)
            PRE = chain.steps
            PER = NORM_STEPS + 1 + 2

            def pair(n):
                chain = Chain(n * PER + PRE)
                for k in range(UNITS):
                    probs_T(n, k)
                    if k < UNITS - 2:
                        score_max(n, k + 2)
                    else:
                        score_max(n + 1, k + 2 - UNITS)
                    if k == 0:
                        prep_T(chain, n + 1, True)
                    if k == 2:
                        values(n + 1)
                    if k == 3:
                        dve.wait_ge(s_x2, 2 * n)
                        dve.wait_ge(s_xn2T, n)
                        dve.wait_ge(s_rows, n)
                        norms(chain, n + 2, n - 1, n)
                    if k == 5:
                        normalise(chain, n, 0)
                    if k == 7:
                        residual(n, 0)
                normalise(chain, n, 1)
                logits(n)
                residual(n, 1)
                assert chain.steps == PER

            with dve.Fori(0, 2) as n:
                pair(n)
            dve.wait_ge(ld_x[1], 16)
            with dve.Fori(2, NPAIR) as n:
                pair(n)
            chain = Chain(NPAIR * PER + PRE)
            dve.wait_ge(s_x2, 2 * NPAIR)
            dve.wait_ge(s_xn2T, NPAIR)
            dve.wait_ge(s_rows, NPAIR)
            norms(chain, None, NPAIR - 1, 0)
            logits(NPAIR)
            dve.wait_ge(s_lg_sb, NPAIR + 1)
            PRE2 = NPAIR * PER + PRE + chain.steps
            dve.wait_ge(c_pool, 10)
            ROUTE_STEPS = 19

            def route(g):
                chain = Chain(g * ROUTE_STEPS + PRE2)
                lg = logits_sb[:, bass.ds(2 + g * GROUP, GROUP), :]

                def over_e(a):
                    return a.unsqueeze(2).to_broadcast([P, GROUP, E])

                rank = erank[:, :].unsqueeze(1).to_broadcast([P, GROUP, E])
                chain.then(nc.vector.tensor_reduce(r_m[:, :], lg, AX.X, ALU.max))
                chain.then(nc.vector.tensor_tensor(out=r_sh[:, :, :], in0=lg, in1=over_e(r_m[:, :]), op=ALU.subtract))
                nc.vector.tensor_scalar(r_sh[:, :, :], r_sh[:, :, :], LOWEST, None, ALU.max).then_inc(s_shift, 1)
                dve.wait_ge(s_shift, g + 1)
                for k in range(2):
                    if k == 0:
                        chain.then(nc.vector.tensor_scalar(r_t[:, :, :], r_sh[:, :, :], 0.0, None, ALU.is_equal))
                    else:
                        chain.then(nc.vector.scalar_tensor_tensor(
                            out=r_pos[:, :, :], in0=r_oh[:, 0, :, :], scalar=-1.0e9, in1=r_sh[:, :, :],
                            op0=ALU.mult, op1=ALU.add))
                        chain.then(nc.vector.tensor_reduce(r_m[:, :], r_pos[:, :, :], AX.X, ALU.max))
                        chain.then(nc.vector.tensor_tensor(out=r_t[:, :, :], in0=r_pos[:, :, :],
                                                           in1=over_e(r_m[:, :]), op=ALU.is_equal))
                    chain.then(nc.vector.tensor_tensor(out=r_t[:, :, :], in0=r_t[:, :, :], in1=rank, op=ALU.mult))
                    chain.then(nc.vector.tensor_reduce(r_m[:, :], r_t[:, :, :], AX.X, ALU.max))
                    chain.then(nc.vector.tensor_tensor(out=r_oh[:, k, :, :], in0=rank,
                                                       in1=over_e(r_m[:, :]), op=ALU.is_equal))
                nc.vector.tensor_tensor(out=r_sel[:, 0:GROUP, :], in0=r_oh[:, 0, :, :], in1=r_oh[:, 1, :, :],
                                        op=ALU.add).then_inc(s_sel, 1)
                dve.wait_ge(s_rexp, g + 1)
                chain.then(nc.vector.tensor_reduce(r_m[:, :], r_ex[:, :, :], AX.X, ALU.add))
                chain.then(nc.vector.reciprocal(r_m[:, :], r_m[:, :]))
                nc.vector.tensor_tensor(out=rows_sb[:, bass.ds(2 + g * GROUP, GROUP), D:D + E], in0=r_ex[:, :, :],
                                        in1=over_e(r_m[:, :]), op=ALU.mult)
                dve.wait_ge(s_pos, g + 1)
                pos = misc[:, 0:(GROUP + 1) * E].rearrange("p (t e) -> p t e", e=E)
                chain.then(nc.vector.tensor_tensor(out=r_pos[:, :, :], in0=pos[:, 0:GROUP, :],
                                                   in1=r_cnt[:, :].unsqueeze(1).to_broadcast([P, GROUP, E]), op=ALU.add))
                nc.vector.tensor_tensor(out=r_cnt[:, :], in0=pos[:, GROUP, :], in1=r_cnt[:, :], op=ALU.add)
                chain.then(nc.vector.tensor_scalar(r_t[:, :, :], r_pos[:, :, :], float(CAP), float(1 << 20),
                                                   ALU.is_ge, ALU.mult))
                chain.then(nc.vector.tensor_tensor(out=r_pos[:, :, :], in0=r_pos[:, :, :], in1=r_t[:, :, :], op=ALU.add))
                chain.then(nc.vector.tensor_tensor(out=r_pos[:, :, :], in0=r_pos[:, :, :],
                                                   in1=eslot[:, :].unsqueeze(1).to_broadcast([P, GROUP, E]), op=ALU.add))
                for k in range(2):
                    last = nc.vector.tensor_tensor(out=r_oh[:, k, :, :], in0=r_oh[:, k, :, :], in1=r_pos[:, :, :], op=ALU.mult)
                chain.then(last)
                dve.wait_ge(s_scat, 16 * TOPK * GROUP * g)
                for k in range(2):
                    last = nc.vector.tensor_reduce(slot_id[:, k, :], r_oh[:, k, :, :], AX.X, ALU.max)
                last.then_inc(s_slot, 1)
                dve.wait_ge(s_slot, g + 1)
                return chain.steps

            with dve.Fori(0, NGROUP) as g:
                steps = route(g)
                assert steps == ROUTE_STEPS

            def slots_T(q, c):
                dve.wait_ge(f_xT, q + 1)
                nc.vector.tensor_copy(xgT[:, c % 2, :], pt_ps[:, :]).then_inc(f_xT_sb, 1)

            def gated(ee, q, c):
                r = c // CHUNKS
                dve.wait_ge(f_y, q + 1)
                if c % 2 == 0:
                    pass
                e = 2 * ee + r
                gate = xg[:, r, (c % CHUNKS) * 4:(c % CHUNKS) * 4 + 4, bass.ds(D + e, 1)]
                return gate

            with dve.Fori(0, E // 2) as ee:
                for c in range(2 * CHUNKS):
                    r, q = c // CHUNKS, ee * 2 * CHUNKS + c
                    if c == 0:
                        dve.wait_ge(ld_g[0], 16 * ee + 16)
                        slots_T(q, c)
                    if c == CHUNKS:
                        dve.wait_ge(ld_g[1], 16 * ee + 16)
                    if c + 1 < 2 * CHUNKS:
                        slots_T(q + 1, c + 1)
                    gate = gated(ee, q, c)
                    dve.wait_ge(f_add[c % 2], 16 * 4 * (ee * CHUNKS + c // 2))
                    nc.vector.tensor_tensor(out=y_sb[:, c % 2, :, :], in0=o_ps[c % 2][:, :].rearrange("p (k d) -> p k d", k=4),
                                            in1=gate.to_broadcast([P, 4, D]), op=ALU.mult).then_inc(f_y_sb, 1)

        @block.tensor
        def _(pe):
            mm = nc.tensor.matmul

            def prep_T(m):
                pe.wait_ge(s_xn, m + 1)
                for s in range(2):
                    last = nc.tensor.transpose(misc[:, s * P:(s + 1) * P], xn[:, s, :], ident[:, :])
                last.then_inc(s_xnT, 1)

            def query_key(m):
                pe.wait_ge(s_xnT_sb, m + 1)
                mm(misc[:, 0:2 * P], wq_sb[:, :], xnT[:, BLK:], start=True, stop=True)
                mm(misc[:, 2 * P:4 * P], wk_sb[:, :], xnT[:, BLK:], start=True, stop=True).then_inc(s_qk, 1)

            def values(m):
                pe.wait_ge(s_qk_sb, m + 1)
                for w in range(4):
                    last = mm(misc[:, w * P:(w + 1) * P], xnT[:, w * BLK:w * BLK + P], wv_sb[:, :], start=True, stop=True)
                last.then_inc(s_v, 1)

            def score(m, k):
                s, blk, half = k // 4, (k // 2) % 2, k % 2
                if k % 4 == 0:
                    pe.wait_ge(s_qbd, 2 * m + s + 1)
                seq_pair = bass.ds(m % PAIRS_PER_SEQ, 1) if s == 0 else slice(1, 2)
                mask = window[:, seq_pair, blk, :].to_broadcast([BLK, 4, P])
                out_ps = scores[k % 4]
                mm(out_ps[:, :].rearrange("p (c j) -> p c j", c=4), blocksel[:, :], mask, start=True, stop=False)
                keys = kT[:, bass.ds(m % 2, 1), s * P + blk * BLK:s * P + blk * BLK + P].rearrange("p o j -> p (o j)")
                for c in range(4):
                    j = 4 * half + c
                    last = mm(out_ps[:, c * P:(c + 1) * P],
                              qbd[s][:, blk, 2 * j:2 * j + 2, :].rearrange("p h q -> p (h q)"), keys,
                              start=False, stop=(c == 3))
                last.then_inc(s_scores, 1)

            def probs_T(n, k):
                pe.wait_ge(s_exp, UNITS * n + k + 1)
                pe.wait_ge(s_pt_sb, UNITS * n + k)
                for c in range(4):
                    last = nc.tensor.transpose(pt_ps[:, c * P:(c + 1) * P], probs[:, k % 2, c, :], ident[:, :])
                last.then_inc(s_pt, 1)

            def weighted(n, k):
                s, blk, half = k // 4, (k // 2) % 2, k % 2
                pe.wait_ge(s_pt_sb, UNITS * n + k + 1)
                if k % 4 == 0:
                    pe.wait_ge(s_v_sb, n + 1)
                    pe.wait_ge(s_x2, 2 * n)
                for c in range(4):
                    j = 4 * half + c
                    v = v_sb[:, bass.ds(n % 2, 1), 2 * s + blk, j, 0:2 * DH + 1].rearrange("p o c -> p (o c)")
                    last = mm(ctx_view(s)[:, blk * HP + j, 0:2 * DH + 1], probsT[:, k % 2, c, :], v, start=True, stop=True)
                last.then_inc(s_pv, 1)

            def context_T(n, s):
                pe.wait_ge(s_ctx, 2 * n + s + 1)
                for blk in range(2):
                    last = nc.tensor.transpose(o_ps[s][:, CTX_T + blk * P:CTX_T + (blk + 1) * P],
                                               ctx_sb[:, s, blk * HP:(blk + 2) * HP, :].rearrange("p j d -> p (j d)"),
                                               ident[:, :])
                last.then_inc(s_ctxT, 1)

            def project(n, s):
                pe.wait_ge(s_ctxT_sb, 2 * n + s + 1)
                for par in range(2):
                    last = mm(o_ps[s][:, ATT:ATT + D], ctxT[:, s, par, :, :].rearrange("p b q -> p (b q)"),
                              wo_sb[:, par, :], start=(par == 0), stop=(par == 1))
                last.then_inc(s_att, 1)

            def router_T(n):
                pe.wait_ge(s_xn2, n + 1)
                for s in range(2):
                    last = nc.tensor.transpose(misc[:, s * P:(s + 1) * P], xn2[:, s, :], ident[:, :])
                last.then_inc(s_xn2T, 1)

            def router(n):
                pe.wait_ge(s_xn2T_sb, n + 1)
                for s in range(2):
                    last = mm(misc[:, s * E:(s + 1) * E], xn2T[:, s * P:(s + 1) * P], wr_sb[:, :], start=True, stop=True)
                last.then_inc(s_lg, 1)

            pe.wait_ge(c_pool, 18)
            pe.wait_ge(c_dve, 1)
            pe.wait_ge(ld_w, 16 * 21)
            prep_T(0)
            query_key(0)
            values(0)
            score(0, 0)
            score(0, 1)
            pe.wait_ge(s_v_sb, 1)
            with pe.Fori(0, NPAIR) as n:
                for k in range(UNITS):
                    probs_T(n, k)
                    if k < UNITS - 2:
                        score(n, k + 2)
                    else:
                        score(n + 1, k + 2 - UNITS)
                    if k > 0:
                        weighted(n, k - 1)
                    if k == 0:
                        pe.wait_ge(s_lg_sb, n)
                        prep_T(n + 1)
                    if k == 1:
                        query_key(n + 1)
                    if k == 2:
                        values(n + 1)
                    if k == 6:
                        context_T(n, 0)
                    if k == 7:
                        project(n, 0)
                weighted(n, UNITS - 1)
                pe.wait_ge(s_v_sb, n + 2)
                router_T(n)
                context_T(n, 1)
                router(n)
                project(n, 1)
            pe.wait_ge(s_lg_sb, NPAIR)
            router_T(NPAIR)
            router(NPAIR)

            pe.wait_ge(s_lg_sb, NPAIR + 1)
            W = (GROUP + 1) * E
            with pe.Fori(0, NGROUP) as g:
                pe.wait_ge(s_sel, g + 1)
                pe.wait_ge(s_slot, g)
                sel = r_sel[:, :, :].rearrange("p t e -> p (t e)")
                mm(misc[:, 0:W], before[:, :], sel, start=True, stop=False)
                for back in range(1, GROUP + 1):
                    last = mm(misc[:, back * E:W], ones[:, :], sel[:, 0:W - back * E], start=False, stop=(back == GROUP))
                last.then_inc(s_pos, 1)

            def slots_T(ee, c):
                r, q = c // CHUNKS, ee * 2 * CHUNKS + c
                if c % CHUNKS == 0:
                    pe.wait_ge(ld_g[r], 16 * ee + 16)
                pe.wait_ge(f_xT_sb, q)
                for k in range(4):
                    last = nc.tensor.transpose(pt_ps[:, k * P:(k + 1) * P],
                                               xg[:, r, (c % CHUNKS) * 4 + k, 0:D], ident[:, :])
                last.then_inc(f_xT, 1)

            def hidden(ee, c):
                r, q = c // CHUNKS, ee * 2 * CHUNKS + c
                if c % CHUNKS == 0:
                    pe.wait_ge(ld_e[r], 32 * ee + 32)
                pe.wait_ge(f_xT_sb, q + 1)
                pe.wait_ge(f_gelu, q * FC)
                for f in range(FC):
                    mm(bank[f][:, :], w1_sb[:, r, f * P:(f + 1) * P], xgT[:, c % 2, :], start=True, stop=True).then_inc(f_h, 1)

            def results(ee, c):
                r, q = c // CHUNKS, ee * 2 * CHUNKS + c
                pe.wait_ge(f_gelu, q * FC + FC)
                if c == 0:
                    pe.wait_ge(f_y_sb, q)
                else:
                    pe.wait_ge(f_y_sb, q - 1)
                for k in range(4):
                    for f in range(FC):
                        last = mm(o_ps[c % 2][:, k * D:(k + 1) * D], hT[:, c % 2, f, k * P:(k + 1) * P],
                                  w2_sb[:, r, f, :], start=(f == 0), stop=(f == FC - 1))
                last.then_inc(f_y, 1)

            pe.wait_ge(s_x2, 2 * NPAIR)
            pe.wait_ge(s_max, UNITS * NPAIR + 2)
            with pe.Fori(0, E // 2) as ee:
                slots_T(ee, 0)
                for c in range(2 * CHUNKS):
                    hidden(ee, c)
                    if c + 1 < 2 * CHUNKS:
                        slots_T(ee, c + 1)
                    if c > 0:
                        results(ee, c - 1)
                results(ee, 2 * CHUNKS - 1)


_INS = ["L0_attn_x", "L0_attn_Wq", "L0_attn_Wk", "L0_attn_Wv", "L0_attn_Wo", "L0_ffn_w_router",
        "L0_ffn_w1", "L0_ffn_w2", "L0_ffn_bias"]


def kernel(**inputs):
    import numpy as _np
    import concourse.bacc as _bacc
    from concourse import mybir as _mybir
    from concourse.bass_utils import run_bass_kernel_spmd as _run

    nc = _bacc.Bacc("TRN2", target_bir_lowering=False, num_devices=1)
    arrays, args = {}, []
    for name in _INS:
        a = _np.ascontiguousarray(inputs[name])
        arrays[f"in_{name}"] = a
        args.append(nc.dram_tensor(f"in_{name}", a.shape, _mybir.dt.from_np(a.dtype), kind="ExternalInput").ap())
    out = nc.dram_tensor("out_0", (T + CAP, D), _mybir.dt.float32, kind="ExternalOutput").ap()
    moe_block_kernel(nc, *args, out)
    r = _run(nc, [arrays], core_ids=[0])
    return r.results[0]["out_0"][0:T].reshape(BATCH, SEQ, D)
```

```python
import concourse.bass as bass
from concourse import mybir
from contextlib import ExitStack

F32 = mybir.dt.float32
BF16 = mybir.dt.bfloat16
I32 = mybir.dt.int32
U32 = mybir.dt.uint32
ALU = mybir.AluOpType
ACT = mybir.ActivationFunctionType
AX = mybir.AxisListType

BATCH, SEQ, D = 8, 1024, 128
H, DH, WIN = 16, 8, 64
E, TOPK, F = 8, 2, 512
T = BATCH * SEQ
CAP = TOPK * T // E
P = 128
NTILE = T // P
NPAIR = NTILE // 2
PAIRS_PER_SEQ = SEQ // (2 * P)
GROUP = SEQ // P
NGROUP = NTILE // GROUP
BLK = WIN
UNITS = 8
HP = H // 2
QUADS = 4
HQ = H // QUADS
VW = 2 * DH + 2
ROW = D + E + 1
SPP = CAP // P
LEAD = 3
NEG = -1.0e30
EPS = 1e-5
MAGIC = float(0x5F3759DF)
LOWEST = -104.0
FC = F // P
START = 1
CHUNKS = SPP // 4
ADDED = 16 * 4 * CHUNKS // 2


def moe_block_kernel(nc, x, wq, wk, wv, wo, w_router, w1, w2, bias, out):
    ctx = ExitStack()
    with ctx:
        def sb(name, shape, dt=F32):
            return ctx.enter_context(nc.sbuf_tensor(name, shape, dt))

        def sem(name):
            return ctx.enter_context(nc.semaphore(name))

        slots_dram = nc.dram_tensor("slots_dram", (E * CAP, ROW), F32, kind="Internal").ap()

        x_sb = sb("x_sb", [P, 2 * (NPAIR + 3), D])
        rows_sb = sb("rows_sb", [P, 2 * (NPAIR + 1), ROW])
        logits_sb = sb("logits_sb", [P, 2 * (NPAIR + 1), E])
        wq_sb = sb("wq_sb", [P, D])
        wk_sb = sb("wk_sb", [P, D])
        wv_sb = sb("wv_sb", [P, D])
        wo_sb = sb("wo_sb", [HP * DH, 2, D])
        wr_sb = sb("wr_sb", [P, E])
        bias_sb = sb("bias_sb", [P, D])
        ident = sb("ident", [P, P])
        headmask = sb("headmask", [P, H])
        quadmask = sb("quadmask", [P, HQ])
        blocksel = sb("blocksel", [BLK, P], BF16)
        window = sb("window", [BLK, PAIRS_PER_SEQ, 2, P], BF16)
        before = sb("before", [P, P], BF16)
        ones = sb("ones", [P, P], BF16)
        erank = sb("erank", [P, E])
        eslot = sb("eslot", [P, E])
        empty_rows = sb("empty_rows", [P, SPP, ROW])
        scratch = sb("scratch", [P, 16])
        stats = sb("stats", [P, 4, 6])
        meanvar = sb("meanvar", [P, 4, 2])
        veps = sb("veps", [P, 4])
        rs_i = sb("rs_i", [P, 4], I32)
        rs_a = sb("rs_a", [P, 4])
        rs_y = sb("rs_y", [P, 4])
        xn = sb("xn", [P, 2, D])
        xn2 = sb("xn2", [P, 2, D])
        xn2T = sb("xn2T", [P, 2 * P])
        xnT = sb("xnT", [P, BLK + 2 * P])
        qT = sb("qT", [P, 2, 2 * P])
        kT = sb("kT", [P, 2, QUADS, BLK + 2 * P])
        v_sb = sb("v_sb", [P, 2, 4, HP, VW])
        qbd = [sb(f"qbd{s}", [P, 2, HQ, BLK]) for s in range(2)]
        negmax = sb("negmax", [P, 4, 4])
        probs = sb("probs", [P, 4, 4, P])
        probsT = sb("probsT", [P, 2, 4, P])
        rden = sb("rden", [P, 2, 2 * HP])
        ctx_sb = sb("ctx_sb", [P, 2, 3 * HP, DH])
        ctxT = sb("ctxT", [HP * DH, 2, 2, 2, BLK])
        xbias = sb("xbias", [P, 2, 2, D])
        r_m = sb("r_m", [P, GROUP])
        r_sh = sb("r_sh", [P, GROUP, E])
        r_ex = sb("r_ex", [P, GROUP, E])
        r_t = sb("r_t", [P, GROUP, E])
        r_oh = sb("r_oh", [P, 2, GROUP, E])
        r_sel = sb("r_sel", [P, GROUP + 1, E], BF16)
        r_pos = sb("r_pos", [P, GROUP, E])
        r_cnt = sb("r_cnt", [P, E])
        send_rows = sb("send_rows", [P, GROUP, ROW])
        slot_id = sb("slot_id", [P, 2, GROUP], I32)
        w1_sb = sb("w1_sb", [P, 2, F])
        w2_sb = sb("w2_sb", [P, 2, FC, D])
        xg = sb("xg", [P, 2, SPP, ROW])
        xgT = sb("xgT", [P, 2, 4 * P])
        hT = sb("hT", [P, 2, FC, 4 * P])
        y_sb = sb("y_sb", [P, 2, 4, D])

        bank = [ctx.enter_context(nc.psum_tensor(f"bank{i}", [P, 512], F32)) for i in range(8)]
        scores = bank[0:4]
        pt_ps = bank[4]
        o_ps = bank[5:7]
        misc = bank[7]
        CTX_T, ATT = 0, 256

        def ctx_view(s):
            return o_ps[s][:, 0:2 * HP * VW].rearrange("p (j c) -> p j c", c=VW)

        ld_w = sem("ld_w")
        ld_x = [sem(f"ld_x{i}") for i in range(2)]
        c_pool = sem("c_pool")
        c_dve = sem("c_dve")
        dve_chain = sem("dve_chain")
        d_init = sem("d_init")
        s_xn = sem("s_xn")
        s_xn2 = sem("s_xn2")
        s_xnT = sem("s_xnT")
        s_xnT_sb = sem("s_xnT_sb")
        s_qk = sem("s_qk")
        s_q_sb = sem("s_q_sb")
        s_k01_sb = sem("s_k01_sb")
        s_k23_sb = sem("s_k23_sb")
        s_v = sem("s_v")
        s_v_sb = sem("s_v_sb")
        s_qbd = sem("s_qbd")
        s_scores = sem("s_scores")
        s_max = sem("s_max")
        s_exp = sem("s_exp")
        s_pt = sem("s_pt")
        s_pt_sb = sem("s_pt_sb")
        s_pv = sem("s_pv")
        s_ctx = sem("s_ctx")
        s_ctxT = sem("s_ctxT")
        s_ctxT_sb = sem("s_ctxT_sb")
        s_att = sem("s_att")
        s_x2 = sem("s_x2")
        s_xn2T = sem("s_xn2T")
        s_xn2T_sb = sem("s_xn2T_sb")
        s_lg = sem("s_lg")
        s_lg_sb = sem("s_lg_sb")
        s_rows = sem("s_rows")
        s_xbias = sem("s_xbias")
        s_out = sem("s_out")
        s_shift = sem("s_shift")
        s_rexp = sem("s_rexp")
        s_sel = sem("s_sel")
        s_pos = sem("s_pos")
        s_pos_sb = sem("s_pos_sb")
        s_slot = sem("s_slot")
        s_send = sem("s_send")
        s_turn_sp = sem("s_turn_sp")
        s_turn_pool = sem("s_turn_pool")
        s_turn_dve = sem("s_turn_dve")
        s_scat = sem("s_scat")
        s_sent = sem("s_sent")
        ld_e = [sem(f"ld_e{i}") for i in range(2)]
        ld_g = [sem(f"ld_g{i}") for i in range(2)]
        f_xT = sem("f_xT")
        f_xT_sb = sem("f_xT_sb")
        f_h = sem("f_h")
        f_gelu = sem("f_gelu")
        f_y = sem("f_y")
        f_y_sb = sem("f_y_sb")
        f_add = [sem(f"f_add{i}") for i in range(2)]
        f_added = sem("f_added")

        block = ctx.enter_context(nc.Block())

        def walk(engine, pair):
            with engine.Fori(0, PAIRS_PER_SEQ) as n:
                pair(n)
            with engine.Fori(1, BATCH) as b:
                pair(b * PAIRS_PER_SEQ)
                pair(b * PAIRS_PER_SEQ + 1, b - 1)
                with engine.Fori(2, PAIRS_PER_SEQ) as i:
                    pair(b * PAIRS_PER_SEQ + i)

        @block.sync
        def _(sp):
            xr = x.rearrange("b (s p) d -> p (b s) d", p=P)
            sp.dma_start(x_sb[:, 2:2 + 16, :], xr[:, 0:16, :]).then_inc(ld_x[0], 16)
            for src, dst in ((wq, wq_sb), (wk, wk_sb), (wv, wv_sb), (w_router, wr_sb)):
                sp.dma_start(dst[:, :], src).then_inc(ld_w, 16)
            wo4 = wo.rearrange("(j two d) n -> two j d n", two=2, d=DH)
            for two in range(2):
                for j in range(HP):
                    sp.dma_start(wo_sb[j * DH:(j + 1) * DH, two, :], wo4[two, j]).then_inc(ld_w, 16)
            sp.dma_start(bias_sb[:, :], bias.rearrange("a b d -> (a b) d").to_broadcast([P, D])).then_inc(ld_w, 16)
            sp.dma_start(x_sb[:, 18:2 + NTILE, :], xr[:, 16:NTILE, :]).then_inc(ld_x[1], 16)
            sp.wait_ge(c_pool, 2)
            for e in range(E):
                sp.dma_start(slots_dram[e * CAP:(e + 1) * CAP, :].rearrange("(p j) w -> p (j w)", p=P),
                             empty_rows[:, :, :].rearrange("p j w -> p (j w)")).then_inc(d_init, 16)
            sp.dma_start(out[T:T + CAP, :].rearrange("(p j) w -> p j w", p=P),
                         empty_rows[:, :, 0:D]).then_inc(d_init, 16)
            out_tiles = out[0:T, :].rearrange("(t p) d -> p t d", p=P)

            def keep_rows(n):
                sp.wait_ge(s_xn2, n + 1)
                sp.dma_start(rows_sb[:, bass.ds(2 * n, 2), 0:D], xn2[:, :, :]).then_inc(s_rows, 16)

            def stage(g, n):
                sp.wait_ge(s_rows, START + 16 * (n + 1))
                sp.sem_inc(s_turn_sp, 1)
                sp.wait_ge(s_slot, g + 1)
                sp.dma_start(send_rows[:, :, :],
                             rows_sb[:, bass.ds(2 + g * GROUP, GROUP), :]).then_inc(s_send, 16)

            def pair(n, g=None):
                keep_rows(n)
                if g is not None:
                    stage(g, n)
                sp.wait_ge(s_xbias, n + 1)
                sp.dma_start(out_tiles[:, bass.ds(2 * n, 2), :],
                             xbias[:, bass.ds(n % 2, 1)].rearrange("p o s d -> p (o s) d")).then_inc(s_out, 16)

            walk(sp, pair)
            keep_rows(NPAIR)
            stage(NGROUP - 1, NPAIR)
            slots_e = slots_dram.rearrange("(e p j) w -> p e (j w)", e=E, p=P)
            w1_e = w1.rearrange("e h f -> h e f")
            w2_e = w2.rearrange("e (c p) h -> p e c h", p=P)
            sp.wait_ge(s_out, START + 16 * NPAIR)
            sp.wait_ge(d_init, 16 * (E + 1))
            sp.wait_ge(s_scat, 16 * TOPK * NTILE)

            def load_expert(e, r):
                sp.dma_start(w1_sb[:, r:r + 1, :], w1_e[:, bass.ds(e, 1), :]).then_inc(ld_e[r], 16)
                sp.dma_start(w2_sb[:, r:r + 1, :, :], w2_e[:, bass.ds(e, 1)]).then_inc(ld_e[r], 16)
                sp.dma_start(xg[:, r:r + 1, :, :].rearrange("p o j w -> p o (j w)"),
                             slots_e[:, bass.ds(e, 1), :]).then_inc(ld_g[r], 16)

            load_expert(0, 0)
            load_expert(1, 1)
            with sp.Fori(1, E // 2) as ee:
                for r in range(2):
                    for i in range(2):
                        sp.wait_ge(f_add[i], ADDED * (2 * ee - 1 + r))
                        sp.sem_inc(s_turn_sp, 1)
                    load_expert(2 * ee + r, r)

        @block.gpsimd
        def _(pool):
            pool.memset(empty_rows[:, :, :], 0.0).then_inc(c_pool, 1)
            pool.wait_ge(c_pool, 1)
            pool.iota(empty_rows[:, :, ROW - 1].bitcast(I32), pattern=[[1, SPP]], base=T,
                      channel_multiplier=SPP).then_inc(c_pool, 1)
            pool.memset(ident[:, :], 0.0).then_inc(c_pool, 1)
            pool.memset(blocksel[:, :], 0.0).then_inc(c_pool, 1)
            pool.memset(window[:, :, :, :], 0.0).then_inc(c_pool, 1)
            pool.memset(before[:, :], 1.0).then_inc(c_pool, 1)
            pool.memset(headmask[:, :], 1.0).then_inc(c_pool, 1)
            pool.iota(rows_sb[:, 2:2 + NTILE, ROW - 1].bitcast(I32), pattern=[[P, NTILE]], base=0,
                      channel_multiplier=1).then_inc(c_pool, 1)
            pool.iota(erank[:, :], pattern=[[-1, E]], base=E, channel_multiplier=0,
                      allow_small_or_imprecise_dtypes=True).then_inc(c_pool, 1)
            pool.iota(eslot[:, :], pattern=[[CAP, E]], base=0, channel_multiplier=0,
                      allow_small_or_imprecise_dtypes=True).then_inc(c_pool, 1)
            pool.wait_ge(c_pool, 10)
            pool.affine_select(out=ident[:, :], in_=ident[:, :], compare_op=ALU.not_equal, fill=1.0, base=0,
                               pattern=[[-1, P]], channel_multiplier=1).then_inc(c_pool, 1)
            pool.affine_select(out=blocksel[:, :], in_=blocksel[:, :], compare_op=ALU.not_equal, fill=1.0,
                               base=0, pattern=[[0, 2], [-1, BLK]], channel_multiplier=1).then_inc(c_pool, 1)
            pool.affine_select(out=window[:, :, :, :], in_=window[:, :, :, :], compare_op=ALU.is_gt, fill=NEG,
                               base=0, pattern=[[0, PAIRS_PER_SEQ], [0, 2], [1, P]],
                               channel_multiplier=-1).then_inc(c_pool, 1)
            pool.affine_select(out=before[:, :], in_=before[:, :], compare_op=ALU.is_gt, fill=0.0, base=0,
                               pattern=[[1, P]], channel_multiplier=-1).then_inc(c_pool, 1)
            pool.affine_select(out=headmask[:, :], in_=headmask[:, :], compare_op=ALU.is_ge, fill=0.0, base=0,
                               pattern=[[-DH, H]], channel_multiplier=1).then_inc(c_pool, 1)
            pool.wait_ge(c_pool, 15)
            pool.affine_select(out=window[:, :, :, :], in_=window[:, :, :, :], compare_op=ALU.is_ge, fill=NEG,
                               base=WIN, pattern=[[0, PAIRS_PER_SEQ], [0, 2], [-1, P]],
                               channel_multiplier=1).then_inc(c_pool, 1)
            pool.affine_select(out=headmask[:, :], in_=headmask[:, :], compare_op=ALU.is_ge, fill=0.0,
                               base=DH - 1, pattern=[[DH, H]], channel_multiplier=-1).then_inc(c_pool, 1)
            pool.wait_ge(c_pool, 17)
            pool.memset(window[:, 0, 0, 0:BLK], NEG).then_inc(c_pool, 1)

            def spread_queries(m, s):
                q = qT[:, bass.ds(m % 2, 1), s * P:(s + 1) * P].rearrange("p o (b q) -> p (o b) q", b=2)
                pool.tensor_tensor(out=qbd[s][:, :, :, :],
                                   in0=q.unsqueeze(2).to_broadcast([P, 2, HQ, BLK]),
                                   in1=quadmask[:, :].unsqueeze(1).unsqueeze(3).to_broadcast([P, 2, HQ, BLK]),
                                   op=ALU.mult).then_inc(s_qbd, 1)

            def send(g, tiles):
                pool.wait_ge(s_send, 16 * g + 16)
                pool.sem_inc(s_turn_pool, 1)
                for j in tiles:
                    for k in range(2):
                        pool.indirect_dma_start(
                            out=slots_dram,
                            out_offset=bass.IndirectOffsetOnAxis(ap=slot_id[:, k, j:j + 1].bitcast(U32), axis=0),
                            in_=send_rows[:, j, :],
                            in_offset=None, bounds_check=E * CAP - 1, oob_is_err=False).then_inc(s_scat, 16)

            def pair(n):
                pool.wait_ge(s_q_sb, n + 2)
                pool.wait_ge(s_scores, UNITS * n + 4)
                spread_queries(n + 1, 0)
                pool.wait_ge(s_scores, UNITS * n + 8)
                spread_queries(n + 1, 1)

            def leave(n):
                pool.wait_ge(s_x2, START + 2 * n + 2)
                pool.wait_ge(s_out, START + 16 * n)
                pool.tensor_tensor(out=xbias[:, bass.ds(n % 2, 1)].rearrange("p o s d -> p (o s) d"),
                                   in0=x_sb[:, bass.ds(2 * n + 2, 2), :],
                                   in1=bias_sb[:, :].unsqueeze(1).to_broadcast([P, 2, D]),
                                   op=ALU.add).then_inc(s_xbias, 1)

            pool.wait_ge(c_dve, 2)
            pool.wait_ge(s_q_sb, 1)
            spread_queries(0, 0)
            spread_queries(0, 1)
            pool.wait_ge(ld_w, 16 * 21)
            with pool.Fori(0, PAIRS_PER_SEQ) as n:
                pair(n)
                leave(n)
            pool.wait_ge(d_init, 16 * (E + 1))
            with pool.Fori(1, BATCH) as b:
                for i in range(PAIRS_PER_SEQ):
                    n = b * PAIRS_PER_SEQ + i
                    pair(n)
                    if i >= 2:
                        send(b - 1, range((i - 2) * GROUP // 2, (i - 1) * GROUP // 2))
                    leave(n)
                pool.wait_ge(s_scat, 16 * TOPK * GROUP * b)
                pool.sem_inc(s_sent, 1)
            send(NGROUP - 1, range(GROUP))

            def add_results(ee, r):
                for c in range(CHUNKS):
                    pool.wait_ge(f_y_sb, 2 + (2 * ee + r) * CHUNKS + c + 1)
                    pool.sem_inc(s_turn_pool, 1)
                    pool.wait_ge(d_init, 16 * (E + 1))
                    for k in range(4):
                        pool.indirect_dma_start(
                            out=out,
                            out_offset=bass.IndirectOffsetOnAxis(
                                ap=xg[:, r, 4 * c + k, ROW - 1:ROW].bitcast(U32), axis=0),
                            in_=y_sb[:, c % 2, k, :],
                            in_offset=None, bounds_check=T + CAP - 1, oob_is_err=True,
                            compute_op=ALU.add).then_inc(f_add[c % 2], 16)
                pool.wait_ge(f_add[0], ADDED * (2 * ee + r + 1))
                pool.sem_inc(s_turn_pool, 1)
                pool.wait_ge(f_add[1], ADDED * (2 * ee + r + 1))
                pool.sem_inc(f_added, 1)

            pool.wait_ge(s_out, START + 16 * NPAIR)
            with pool.Fori(0, E // 2) as ee:
                for r in range(2):
                    add_results(ee, r)

        @block.scalar
        def _(act):
            def query_key(m):
                act.wait_ge(s_qk, m + 1)
                nc.scalar.activation(qT[:, bass.ds(m % 2, 1), :].rearrange("p o q -> p (o q)"),
                                     misc[:, 0:2 * P], ACT.Copy, scale=float(DH) ** -0.5).then_inc(s_q_sb, 1)
                for g in range(QUADS // 2):
                    q = slice(32 * g, 32 * g + 32)
                    last = nc.scalar.activation(kT[q, bass.ds(m % 2, 1), g, BLK:].rearrange("p o j -> p (o j)"),
                                                misc[q, 2 * P:4 * P], ACT.Copy)
                last.then_inc(s_k01_sb, 1)

            def query_key_next(n):
                act.wait_ge(s_k01_sb, n + 1)
                act.wait_ge(s_k23_sb, n + 1)
                nc.scalar.activation(kT[:, bass.ds((n + 1) % 2, 1), :, 0:BLK].rearrange("p o g j -> p (o g) j"),
                                     kT[:, bass.ds(n % 2, 1), :, 2 * P:].rearrange("p o g j -> p (o g) j"), ACT.Copy)
                query_key(n + 1)

            def values(m):
                act.wait_ge(s_v, m + 1)
                nc.scalar.activation(v_sb[:, bass.ds(m % 2, 1), :, :, 0:2 * DH].rearrange("p o w j c -> p (o w) j c"),
                                     misc[:, :].rearrange("p (w j c) -> p w j c", w=4, j=HP), ACT.Copy).then_inc(s_v_sb, 1)

            def exps(n, k):
                act.wait_ge(s_max, UNITS * n + k + 1)
                for c in range(4):
                    last = nc.scalar.activation(probs[:, k % 4, c, :], scores[k % 4][:, c * P:(c + 1) * P], ACT.Exp,
                                                bias=negmax[:, k % 4, c:c + 1])
                last.then_inc(s_exp, 1)

            def context_T(n, s):
                act.wait_ge(s_ctxT, 2 * n + s + 1)
                nc.scalar.activation(ctxT[:, s, :, :, :],
                                     o_ps[s][0:HP * DH, CTX_T:CTX_T + 2 * P].rearrange(
                                         "p (b h q) -> p h b q", b=2, h=2), ACT.Copy).then_inc(s_ctxT_sb, 1)

            def router_T(n):
                act.wait_ge(s_xn2T, START + n + 1)
                nc.scalar.activation(xn2T[:, :], misc[:, 0:2 * P], ACT.Copy).then_inc(s_xn2T_sb, 1)

            def gate_exps(g):
                act.wait_ge(s_shift, g + 1)
                nc.scalar.activation(r_ex[:, :, :], r_sh[:, :, :], ACT.Exp).then_inc(s_rexp, 1)

            def pair(n, g=None):
                for k in range(UNITS):
                    exps(n, k)
                    if k == 3:
                        query_key_next(n)
                    if k == 5:
                        values(n + 1)
                    if k == 4 and g is not None:
                        gate_exps(g)
                    if k == 7:
                        context_T(n, 0)
                router_T(n)
                context_T(n, 1)

            act.wait_ge(c_dve, 2)
            query_key(0)
            values(0)
            walk(act, pair)
            router_T(NPAIR)
            gate_exps(NGROUP - 1)

            with act.Fori(0, E // 2) as ee:
                for c in range(2 * CHUNKS):
                    for f in range(FC):
                        act.wait_ge(f_h, (ee * 2 * CHUNKS + c) * FC + f + 1)
                        nc.scalar.activation(hT[:, c % 2, f, :], bank[f][:, :], ACT.Gelu_apprx_tanh).then_inc(f_gelu, 1)

        @block.vector
        def _(dve):
            class Chain:
                def __init__(self, base):
                    self.base, self.steps = base, 0

                def mark(self, instruction):
                    instruction.then_inc(dve_chain, 1)
                    self.steps += 1

                def wait(self):
                    dve.wait_ge(dve_chain, self.base + self.steps)

            def norms(chain, first, second, steps):
                tiles = [x_sb[:, bass.ds(2 * a + 2 + s, 1), :].rearrange("p o d -> p (o d)")
                         for a in (first, second) if a is not None for s in range(2)]
                w = len(tiles)
                v, y, a = veps[:, 0:w], rs_y[:, 0:w], rs_a[:, 0:w]
                mean, diff = meanvar[:, 0:w, 0], meanvar[:, 0:w, 1]
                for step in steps:
                    if step > 0:
                        chain.wait()
                    if step == 0:
                        for i, t in enumerate(tiles):
                            last = nc.vector.bn_stats(stats[:, i, :], t)
                        chain.mark(last)
                    elif step == 1:
                        nc.vector.tensor_tensor(out=mean, in0=stats[:, 0:w, 1], in1=stats[:, 0:w, 4], op=ALU.add)
                        nc.vector.tensor_tensor(out=v, in0=stats[:, 0:w, 2], in1=stats[:, 0:w, 5], op=ALU.add)
                        chain.mark(nc.vector.tensor_tensor(out=diff, in0=stats[:, 0:w, 1], in1=stats[:, 0:w, 4],
                                                           op=ALU.subtract))
                    elif step == 2:
                        nc.vector.tensor_scalar(mean, mean, 0.5, None, ALU.mult)
                        nc.vector.tensor_scalar(v, v, 1.0 / D, EPS, ALU.mult, ALU.add)
                        chain.mark(nc.vector.scalar_tensor_tensor(out=diff, in0=diff, scalar=0.25, in1=diff,
                                                                  op0=ALU.mult, op1=ALU.mult))
                    elif step == 3:
                        chain.mark(nc.vector.tensor_tensor(out=v, in0=v, in1=diff, op=ALU.add))
                    elif step == 4:
                        chain.mark(nc.vector.tensor_scalar(rs_i[:, 0:w], v.bitcast(I32), 1, None,
                                                           ALU.logical_shift_right))
                    elif step == 5:
                        chain.mark(nc.vector.tensor_scalar(y.bitcast(I32), rs_i[:, 0:w], -1.0, MAGIC, ALU.mult, ALU.add))
                    elif step < 15 and step % 3 == 0:
                        chain.mark(nc.vector.scalar_tensor_tensor(out=a, in0=y, scalar=-0.5, in1=y,
                                                                  op0=ALU.mult, op1=ALU.mult))
                    elif step < 15 and step % 3 == 1:
                        chain.mark(nc.vector.tensor_tensor(out=a, in0=a, in1=v, op=ALU.mult))
                    elif step < 15:
                        chain.mark(nc.vector.scalar_tensor_tensor(out=y, in0=a, scalar=1.5, in1=y,
                                                                  op0=ALU.add, op1=ALU.mult))
                    else:
                        i = 0
                        for which, dst, done in ((first, xn, s_xn), (second, xn2, s_xn2)):
                            if which is None:
                                continue
                            for s in range(2):
                                last = nc.vector.tensor_scalar(dst[:, s, :], tiles[i], meanvar[:, i, 0:1],
                                                               rs_y[:, i:i + 1], ALU.subtract, ALU.mult)
                                i += 1
                            last.then_inc(done, 1)

            ALL = range(16)

            def prep_T(chain, m, pull):
                dve.wait_ge(s_xnT, m + 1)
                if pull:
                    dve.wait_ge(s_xnT_sb, m)
                    chain.mark(nc.vector.tensor_copy(xnT[:, 0:BLK], xnT[:, 2 * P:]))
                    chain.wait()
                nc.vector.tensor_copy(xnT[:, BLK:], misc[:, 0:2 * P]).then_inc(s_xnT_sb, 1)

            def keys(m):
                dve.wait_ge(s_q_sb, m + 1)
                for g in range(QUADS // 2, QUADS):
                    q = slice(32 * g, 32 * g + 32)
                    last = nc.vector.tensor_copy(kT[q, bass.ds(m % 2, 1), g, BLK:].rearrange("p o j -> p (o j)"),
                                                 misc[q, 2 * P:4 * P])
                last.then_inc(s_k23_sb, 1)

            def score_max(n, k):
                dve.wait_ge(s_scores, UNITS * n + k + 1)
                nc.vector.tensor_reduce(negmax[:, k % 4, :], scores[k % 4][:, :].rearrange("p (c j) -> p c j", c=4),
                                        AX.X, ALU.max, negate=True).then_inc(s_max, 1)

            def probs_T(n, k):
                dve.wait_ge(s_pt, UNITS * n + k + 1)
                nc.vector.tensor_copy(probsT[:, k % 2, :, :].rearrange("p c j -> p (c j)"),
                                      pt_ps[:, :]).then_inc(s_pt_sb, 1)

            def normalise(chain, n, s):
                dve.wait_ge(s_pv, UNITS * n + 4 * s + 4)
                o = ctx_view(s)
                chain.mark(nc.vector.reciprocal(rden[:, s, :], o[:, :, 2 * DH]))
                chain.wait()
                for par in range(2):
                    q = slice(par * BLK, (par + 1) * BLK)
                    last = nc.vector.tensor_tensor(out=ctx_sb[q, s, 0:2 * HP, :], in0=o[q, :, par * DH:(par + 1) * DH],
                                                   in1=rden[q, s, :].unsqueeze(2).to_broadcast([BLK, 2 * HP, DH]),
                                                   op=ALU.mult)
                last.then_inc(s_ctx, 1)

            def residual(n, s):
                dve.wait_ge(s_att, 2 * n + s + 1)
                t = x_sb[:, bass.ds(2 * n + 2 + s, 1), :].rearrange("p o d -> p (o d)")
                nc.vector.tensor_tensor(out=t, in0=o_ps[s][:, ATT:ATT + D], in1=t, op=ALU.add).then_inc(s_x2, 1)

            def logits(n):
                dve.wait_ge(s_lg, n + 1)
                nc.vector.tensor_copy(logits_sb[:, bass.ds(2 * n, 2), :].rearrange("p t e -> p (t e)"),
                                      misc[:, 0:2 * E]).then_inc(s_lg_sb, 1)

            def pick(chain, k, part):
                rank = erank[:, :].unsqueeze(1).to_broadcast([P, GROUP, E])
                over_e = r_m[:, :].unsqueeze(2).to_broadcast([P, GROUP, E])
                chain.wait()
                if part == "others":
                    chain.mark(nc.vector.scalar_tensor_tensor(out=r_pos[:, :, :], in0=r_oh[:, 0, :, :], scalar=-1.0e9,
                                                              in1=r_sh[:, :, :], op0=ALU.mult, op1=ALU.add))
                elif part == "largest":
                    chain.mark(nc.vector.tensor_reduce(r_m[:, :], r_pos[:, :, :], AX.X, ALU.max))
                elif part == "equal":
                    if k == 0:
                        chain.mark(nc.vector.tensor_scalar(r_t[:, :, :], r_sh[:, :, :], 0.0, None, ALU.is_equal))
                    else:
                        chain.mark(nc.vector.tensor_tensor(out=r_t[:, :, :], in0=r_pos[:, :, :], in1=over_e,
                                                           op=ALU.is_equal))
                elif part == "ranks":
                    chain.mark(nc.vector.tensor_tensor(out=r_t[:, :, :], in0=r_t[:, :, :], in1=rank, op=ALU.mult))
                elif part == "first":
                    chain.mark(nc.vector.tensor_reduce(r_m[:, :], r_t[:, :, :], AX.X, ALU.max))
                else:
                    chain.mark(nc.vector.tensor_tensor(out=r_oh[:, k, :, :], in0=rank, in1=over_e, op=ALU.is_equal))

            def shift(chain, g, part):
                lg = logits_sb[:, bass.ds(2 + g * GROUP, GROUP), :]
                if part == 0:
                    chain.mark(nc.vector.tensor_reduce(r_m[:, :], lg, AX.X, ALU.max))
                elif part == 1:
                    chain.wait()
                    chain.mark(nc.vector.tensor_tensor(out=r_sh[:, :, :], in0=lg,
                                                       in1=r_m[:, :].unsqueeze(2).to_broadcast([P, GROUP, E]),
                                                       op=ALU.subtract))
                else:
                    chain.wait()
                    nc.vector.tensor_scalar(r_sh[:, :, :], r_sh[:, :, :], LOWEST, None, ALU.max).then_inc(s_shift, 1)
                    dve.wait_ge(s_shift, g + 1)

            def gates(chain, g, part):
                if part == 0:
                    chain.wait()
                    nc.vector.tensor_tensor(out=r_sel[:, 0:GROUP, :], in0=r_oh[:, 0, :, :], in1=r_oh[:, 1, :, :],
                                            op=ALU.add).then_inc(s_sel, 1)
                    dve.wait_ge(s_rexp, g + 1)
                    chain.mark(nc.vector.tensor_reduce(r_m[:, :], r_ex[:, :, :], AX.X, ALU.add))
                elif part == 1:
                    chain.wait()
                    chain.mark(nc.vector.reciprocal(r_m[:, :], r_m[:, :]))
                else:
                    chain.wait()
                    nc.vector.tensor_tensor(out=rows_sb[:, bass.ds(2 + g * GROUP, GROUP), D:D + E], in0=r_ex[:, :, :],
                                            in1=r_m[:, :].unsqueeze(2).to_broadcast([P, GROUP, E]), op=ALU.mult)

            def positions(chain, g, part):
                if part == 0:
                    dve.wait_ge(s_pos, g + 1)
                    pos = misc[:, 0:(GROUP + 1) * E].rearrange("p (t e) -> p t e", e=E)
                    chain.mark(nc.vector.tensor_tensor(out=r_pos[:, :, :], in0=pos[:, 0:GROUP, :],
                                                       in1=r_cnt[:, :].unsqueeze(1).to_broadcast([P, GROUP, E]),
                                                       op=ALU.add))
                    chain.wait()
                    nc.vector.tensor_tensor(out=r_cnt[:, :], in0=pos[:, GROUP, :], in1=r_cnt[:, :],
                                            op=ALU.add).then_inc(s_pos_sb, 1)
                    return
                chain.wait()
                if part == 1:
                    chain.mark(nc.vector.tensor_scalar(r_t[:, :, :], r_pos[:, :, :], float(CAP), float(1 << 20),
                                                       ALU.is_ge, ALU.mult))
                elif part == 2:
                    chain.mark(nc.vector.tensor_tensor(out=r_pos[:, :, :], in0=r_pos[:, :, :], in1=r_t[:, :, :], op=ALU.add))
                elif part == 3:
                    chain.mark(nc.vector.tensor_tensor(out=r_pos[:, :, :], in0=r_pos[:, :, :],
                                                       in1=eslot[:, :].unsqueeze(1).to_broadcast([P, GROUP, E]), op=ALU.add))
                elif part == 4:
                    for k in range(2):
                        last = nc.vector.tensor_tensor(out=r_oh[:, k, :, :], in0=r_oh[:, k, :, :], in1=r_pos[:, :, :],
                                                       op=ALU.mult)
                    chain.mark(last)
                else:
                    dve.wait_ge(s_sent, START + g)
                    for k in range(2):
                        last = nc.vector.tensor_reduce(slot_id[:, k, :], r_oh[:, k, :, :], AX.X, ALU.max)
                    last.then_inc(s_slot, 1)

            def route(chain, g, at):
                if at == 0:
                    for part in range(3):
                        shift(chain, g, part)
                elif at == 1:
                    for part in ("equal", "ranks", "first", "mark"):
                        pick(chain, 0, part)
                elif at == 2:
                    for part in ("others", "largest", "equal"):
                        pick(chain, 1, part)
                elif at == 3:
                    for part in ("ranks", "first", "mark"):
                        pick(chain, 1, part)
                elif at == 4:
                    for part in range(3):
                        gates(chain, g, part)
                elif at == 7:
                    for part in range(6):
                        positions(chain, g, part)

            nc.vector.memset(x_sb[:, 0:2, :], 0.0)
            nc.vector.memset(x_sb[:, 2 + NTILE:, :], 0.0)
            nc.vector.memset(kT[:, :, :, :], 0.0)
            nc.vector.memset(xnT[:, 0:BLK], 0.0)
            nc.vector.memset(ones[:, :], 1.0)
            nc.vector.memset(ctx_sb[:, :, 2 * HP:, :], 0.0)
            nc.vector.memset(v_sb[:, :, :, :, 2 * DH:], 1.0)
            nc.vector.memset(r_sel[:, GROUP, :], 0.0)
            nc.vector.memset(r_cnt[:, :], 0.0).then_inc(c_dve, 1)
            for i, free in enumerate((s_x2, s_xn2T, s_lg_sb, s_pt_sb, s_rows, s_out, s_sent, f_added)):
                nc.vector.memset(scratch[:, i:i + 1], 0.0).then_inc(free, START)
            nc.vector.memset(scratch[:, 15:16], 0.0).then_inc(f_y_sb, 2)
            dve.wait_ge(c_dve, 1)

            chain = Chain(0)
            dve.wait_ge(ld_x[0], 16)
            norms(chain, 0, None, ALL)
            dve.wait_ge(c_pool, 17)
            nc.vector.tensor_reduce(quadmask[:, :], headmask[:, :].rearrange("p (g h) -> p h g", g=QUADS),
                                    AX.X, ALU.add).then_inc(c_dve, 1)
            prep_T(chain, 0, False)
            keys(0)
            dve.wait_ge(s_xnT, 1)
            norms(chain, 1, None, ALL)
            for k in range(LEAD):
                score_max(0, k)
            PRE = chain.steps
            PER, ROUTE_STEPS = 15 + 1 + 2, 2 + 10 + 2 + 5

            def pair(n, g=None):
                chain = Chain(n * PER + PRE + ROUTE_STEPS * pair.routed)
                for k in range(UNITS):
                    probs_T(n, k)
                    if k == 1:
                        prep_T(chain, n + 1, True)
                    if k > 0:
                        norms(chain, n + 2, n - 1, NORM_AT[2 * k])
                    if k + LEAD < UNITS:
                        score_max(n, k + LEAD)
                    else:
                        score_max(n + 1, k + LEAD - UNITS)
                    if k == 0:
                        dve.wait_ge(s_x2, START + 2 * n)
                    if k == 6:
                        dve.wait_ge(s_xn2T, START + n)
                        dve.wait_ge(s_rows, START + 16 * n)
                        dve.wait_ge(s_xnT, n + 2)
                    norms(chain, n + 2, n - 1, NORM_AT[2 * k + 1])
                    if k == 3:
                        keys(n + 1)
                    if k == 5:
                        normalise(chain, n, 0)
                    if g is not None:
                        route(chain, g, k)
                    if k == 7:
                        residual(n, 0)
                normalise(chain, n, 1)
                logits(n)
                residual(n, 1)
                assert chain.steps == PER + (0 if g is None else ROUTE_STEPS), chain.steps

            NORM_AT = [(), (0,), (1,), (2, 3), (4,), (5, 6), (7,), (8,), (9, 10), (11, 12), (13,), (14,), (), (15,), (), ()]

            pair.routed = 0
            with dve.Fori(0, 2) as n:
                pair(n)
            dve.wait_ge(ld_x[1], 16)
            with dve.Fori(2, PAIRS_PER_SEQ) as n:
                pair(n)
            with dve.Fori(1, BATCH) as b:
                pair.routed = b - 1
                pair(b * PAIRS_PER_SEQ)
                pair(b * PAIRS_PER_SEQ + 1, b - 1)
                pair.routed = b
                with dve.Fori(2, PAIRS_PER_SEQ) as i:
                    pair(b * PAIRS_PER_SEQ + i)
            chain = Chain(NPAIR * PER + PRE + ROUTE_STEPS * (BATCH - 1))
            dve.wait_ge(s_x2, START + 2 * NPAIR)
            dve.wait_ge(s_xn2T, START + NPAIR)
            dve.wait_ge(s_rows, START + 16 * NPAIR)
            norms(chain, None, NPAIR - 1, ALL)
            logits(NPAIR)
            dve.wait_ge(s_lg_sb, START + NPAIR + 1)
            for k in range(UNITS):
                route(chain, NGROUP - 1, k)

            def slots_T(q, c):
                dve.wait_ge(f_xT, q + 1)
                nc.vector.tensor_copy(xgT[:, c % 2, :], pt_ps[:, :]).then_inc(f_xT_sb, 1)

            def gated(ee, q, c):
                r = c // CHUNKS
                if c % CHUNKS == 0:
                    dve.wait_ge(ld_g[r], 16 * ee + 16)
                    dve.sem_inc(s_turn_dve, 1)
                dve.wait_ge(f_y, q + 1)
                if c < 2:
                    dve.wait_ge(f_added, START + 2 * ee)
                else:
                    dve.wait_ge(f_add[c % 2], 16 * 4 * (ee * CHUNKS + c // 2))
                gate = xg[:, r, (c % CHUNKS) * 4:(c % CHUNKS) * 4 + 4, bass.ds(D + 2 * ee + r, 1)]
                nc.vector.tensor_tensor(out=y_sb[:, c % 2, :, :],
                                        in0=o_ps[c % 2][:, :].rearrange("p (k d) -> p k d", k=4),
                                        in1=gate.to_broadcast([P, 4, D]), op=ALU.mult).then_inc(f_y_sb, 1)

            with dve.Fori(0, E // 2) as ee:
                slots_T(ee * 2 * CHUNKS, 0)
                for c in range(2 * CHUNKS):
                    q = ee * 2 * CHUNKS + c
                    if c + 1 < 2 * CHUNKS:
                        slots_T(q + 1, c + 1)
                    if c > 0:
                        gated(ee, q - 1, c - 1)
                gated(ee, ee * 2 * CHUNKS + 2 * CHUNKS - 1, 2 * CHUNKS - 1)

        @block.tensor
        def _(pe):
            mm = nc.tensor.matmul

            def prep_T(m):
                pe.wait_ge(s_xn, m + 1)
                for s in range(2):
                    last = nc.tensor.transpose(misc[:, s * P:(s + 1) * P], xn[:, s, :], ident[:, :])
                last.then_inc(s_xnT, 1)

            def query_key(m):
                pe.wait_ge(s_xnT_sb, m + 1)
                mm(misc[:, 0:2 * P], wq_sb[:, :], xnT[:, BLK:], start=True, stop=True)
                mm(misc[:, 2 * P:4 * P], wk_sb[:, :], xnT[:, BLK:], start=True, stop=True).then_inc(s_qk, 1)

            def values(m):
                pe.wait_ge(s_k01_sb, m + 1)
                pe.wait_ge(s_k23_sb, m + 1)
                for w in range(4):
                    last = mm(misc[:, w * P:(w + 1) * P], xnT[:, w * BLK:w * BLK + P], wv_sb[:, :], start=True, stop=True)
                last.then_inc(s_v, 1)

            def score(m, k):
                s, blk, half = k // 4, (k // 2) % 2, k % 2
                if k % 4 == 0:
                    pe.wait_ge(s_qbd, 2 * m + s + 1)
                if k == 0:
                    pe.wait_ge(s_k01_sb, m + 1)
                    pe.wait_ge(s_k23_sb, m + 1)
                seq_pair = bass.ds(m % PAIRS_PER_SEQ, 1) if s == 0 else slice(1, 2)
                mask = window[:, seq_pair, blk, :].to_broadcast([BLK, 4, P])
                out_ps = scores[k % 4]
                mm(out_ps[:, :].rearrange("p (c j) -> p c j", c=4), blocksel[:, :], mask, start=True, stop=False)
                for c in range(4):
                    j = 4 * half + c
                    h = 2 * j % HQ
                    keys = kT[:, bass.ds(m % 2, 1), 2 * j // HQ, s * P + blk * BLK:s * P + blk * BLK + P]
                    last = mm(out_ps[:, c * P:(c + 1) * P],
                              qbd[s][:, blk, h:h + 2, :].rearrange("p h q -> p (h q)"),
                              keys.rearrange("p o j -> p (o j)"),
                              start=False, stop=(c == 3))
                last.then_inc(s_scores, 1)

            def probs_T(n, k):
                pe.wait_ge(s_exp, UNITS * n + k + 1)
                pe.wait_ge(s_pt_sb, START + UNITS * n + k)
                for c in range(4):
                    last = nc.tensor.transpose(pt_ps[:, c * P:(c + 1) * P], probs[:, k % 4, c, :], ident[:, :])
                last.then_inc(s_pt, 1)

            def weighted(n, k):
                s, blk, half = k // 4, (k // 2) % 2, k % 2
                pe.wait_ge(s_pt_sb, START + UNITS * n + k + 1)
                if k % 4 == 0:
                    pe.wait_ge(s_v_sb, n + 1)
                    pe.wait_ge(s_x2, START + 2 * n)
                for c in range(4):
                    j = 4 * half + c
                    v = v_sb[:, bass.ds(n % 2, 1), 2 * s + blk, j, 0:2 * DH + 1].rearrange("p o c -> p (o c)")
                    last = mm(ctx_view(s)[:, blk * HP + j, 0:2 * DH + 1], probsT[:, k % 2, c, :], v, start=True, stop=True)
                last.then_inc(s_pv, 1)

            def context_T(n, s):
                pe.wait_ge(s_ctx, 2 * n + s + 1)
                for blk in range(2):
                    last = nc.tensor.transpose(o_ps[s][:, CTX_T + blk * P:CTX_T + (blk + 1) * P],
                                               ctx_sb[:, s, blk * HP:(blk + 2) * HP, :].rearrange("p j d -> p (j d)"),
                                               ident[:, :])
                last.then_inc(s_ctxT, 1)

            def project(n, s):
                pe.wait_ge(s_ctxT_sb, 2 * n + s + 1)
                for par in range(2):
                    last = mm(o_ps[s][:, ATT:ATT + D], ctxT[:, s, par, :, :].rearrange("p b q -> p (b q)"),
                              wo_sb[:, par, :], start=(par == 0), stop=(par == 1))
                last.then_inc(s_att, 1)

            def router_T(n):
                pe.wait_ge(s_xn2, n + 1)
                for s in range(2):
                    last = nc.tensor.transpose(misc[:, s * P:(s + 1) * P], xn2[:, s, :], ident[:, :])
                last.then_inc(s_xn2T, 1)

            def router(n):
                pe.wait_ge(s_xn2T_sb, n + 1)
                for s in range(2):
                    last = mm(misc[:, s * E:(s + 1) * E], xn2T[:, s * P:(s + 1) * P], wr_sb[:, :], start=True, stop=True)
                last.then_inc(s_lg, 1)

            pe.wait_ge(c_pool, 18)
            pe.wait_ge(c_dve, 1)
            pe.wait_ge(ld_w, 16 * 21)
            prep_T(0)
            query_key(0)
            values(0)
            for k in range(LEAD):
                score(0, k)
            pe.wait_ge(s_v_sb, 1)

            def counts(g):
                pe.wait_ge(s_sel, g + 1)
                sel = r_sel[:, :, :].rearrange("p t e -> p (t e)")
                W = (GROUP + 1) * E
                mm(misc[:, 0:W], before[:, :], sel, start=True, stop=False)
                for back in range(1, GROUP + 1):
                    last = mm(misc[:, back * E:W], ones[:, :], sel[:, 0:W - back * E], start=False, stop=(back == GROUP))
                last.then_inc(s_pos, 1)

            def pair(n, g=None):
                for k in range(UNITS):
                    probs_T(n, k)
                    if k + LEAD < UNITS:
                        score(n, k + LEAD)
                    else:
                        score(n + 1, k + LEAD - UNITS)
                    if k > 0:
                        weighted(n, k - 1)
                    if k == 0:
                        pe.wait_ge(s_lg_sb, START + n)
                        prep_T(n + 1)
                    if k == 2:
                        query_key(n + 1)
                    if k == 4:
                        values(n + 1)
                    if k == 6:
                        context_T(n, 0)
                        pe.wait_ge(s_v_sb, n + 2)
                        if g is not None:
                            counts(g)
                    if k == 7:
                        project(n, 0)
                weighted(n, UNITS - 1)
                if g is not None:
                    pe.wait_ge(s_pos_sb, g + 1)
                router_T(n)
                context_T(n, 1)
                router(n)
                project(n, 1)

            walk(pe, pair)
            pe.wait_ge(s_lg_sb, START + NPAIR)
            router_T(NPAIR)
            router(NPAIR)
            pe.wait_ge(s_lg_sb, START + NPAIR + 1)
            counts(NGROUP - 1)

            def slots_T(ee, c):
                r, q = c // CHUNKS, ee * 2 * CHUNKS + c
                if c % CHUNKS == 0:
                    pe.wait_ge(ld_g[r], 16 * ee + 16)
                for k in range(4):
                    last = nc.tensor.transpose(pt_ps[:, k * P:(k + 1) * P],
                                               xg[:, r, (c % CHUNKS) * 4 + k, 0:D], ident[:, :])
                last.then_inc(f_xT, 1)

            def hidden(ee, c):
                r, q = c // CHUNKS, ee * 2 * CHUNKS + c
                if c % CHUNKS == 0:
                    pe.wait_ge(ld_e[r], 32 * ee + 32)
                pe.wait_ge(f_xT_sb, q + 1)
                if c > 0:
                    pe.wait_ge(f_gelu, q * FC)
                for f in range(FC):
                    mm(bank[f][:, :], w1_sb[:, r, f * P:(f + 1) * P], xgT[:, c % 2, :], start=True, stop=True).then_inc(f_h, 1)

            def results(ee, c):
                r, q = c // CHUNKS, ee * 2 * CHUNKS + c
                pe.wait_ge(f_gelu, q * FC + FC)
                pe.wait_ge(f_y_sb, q + 1)
                for k in range(4):
                    for f in range(FC):
                        last = mm(o_ps[c % 2][:, k * D:(k + 1) * D], hT[:, c % 2, f, k * P:(k + 1) * P],
                                  w2_sb[:, r, f, :], start=(f == 0), stop=(f == FC - 1))
                last.then_inc(f_y, 1)

            pe.wait_ge(s_x2, START + 2 * NPAIR)
            pe.wait_ge(s_max, UNITS * NPAIR + LEAD)
            with pe.Fori(0, E // 2) as ee:
                slots_T(ee, 0)
                for c in range(2 * CHUNKS):
                    hidden(ee, c)
                    if c + 1 < 2 * CHUNKS:
                        slots_T(ee, c + 1)
                    if c > 0:
                        results(ee, c - 1)
                results(ee, 2 * CHUNKS - 1)


_INS = ["L0_attn_x", "L0_attn_Wq", "L0_attn_Wk", "L0_attn_Wv", "L0_attn_Wo", "L0_ffn_w_router",
        "L0_ffn_w1", "L0_ffn_w2", "L0_ffn_bias"]


def kernel(**inputs):
    import numpy as _np
    import concourse.bacc as _bacc
    from concourse import mybir as _mybir
    from concourse.bass_utils import run_bass_kernel_spmd as _run

    nc = _bacc.Bacc("TRN2", target_bir_lowering=False, num_devices=1)
    arrays, args = {}, []
    for name in _INS:
        a = _np.ascontiguousarray(inputs[name])
        arrays[f"in_{name}"] = a
        args.append(nc.dram_tensor(f"in_{name}", a.shape, _mybir.dt.from_np(a.dtype), kind="ExternalInput").ap())
    out = nc.dram_tensor("out_0", (T + CAP, D), _mybir.dt.float32, kind="ExternalOutput").ap()
    moe_block_kernel(nc, *args, out)
    r = _run(nc, [arrays], core_ids=[0])
    return r.results[0]["out_0"][0:T].reshape(BATCH, SEQ, D)
```

```python
import concourse.bass as bass
from concourse import mybir
from contextlib import ExitStack

F32 = mybir.dt.float32
F32R = mybir.dt.float32r
BF16 = mybir.dt.bfloat16
I32 = mybir.dt.int32
U32 = mybir.dt.uint32
ALU = mybir.AluOpType
ACT = mybir.ActivationFunctionType
AX = mybir.AxisListType

BATCH, SEQ, D = 8, 1024, 128
H, DH, WIN = 16, 8, 64
E, TOPK, F = 8, 2, 512
T = BATCH * SEQ
CAP = TOPK * T // E
P = 128
NTILE = T // P
NPAIR = NTILE // 2
PAIRS_PER_SEQ = SEQ // (2 * P)
GROUP = SEQ // P
NGROUP = NTILE // GROUP
BLK = WIN
UNITS = 8
HP = H // 2
QUADS = 4
HQ = H // QUADS
VW = 2 * DH + 2
ROW = D + E + 1
SPP = CAP // P
BY_ACT = (0, 5)
LEAD = 3
FRONT = 4
NEG = -1.0e30
EPS = 1e-5
MAGIC = float(0x5F3759DF)
LOWEST = -104.0
FC = F // P
ROUTED_AT = PAIRS_PER_SEQ - 2
START = 2
CHUNKS = SPP // 4
ADDED = 16 * 4 * CHUNKS // 2


def moe_block_kernel(nc, x, wq, wk, wv, wo, w_router, w1, w2, bias, out):
    ctx = ExitStack()
    with ctx:
        def sb(name, shape, dt=F32):
            return ctx.enter_context(nc.sbuf_tensor(name, shape, dt))

        def sem(name):
            return ctx.enter_context(nc.semaphore(name))

        slots_dram = nc.dram_tensor("slots_dram", (E * CAP, ROW), F32, kind="Internal").ap()

        rows_sb = sb("rows_sb", [P, FRONT + NTILE, ROW])
        logits_sb = sb("logits_sb", [P, FRONT + NTILE, E])
        wq_sb = sb("wq_sb", [P, D])
        wk_sb = sb("wk_sb", [P, D])
        wv_sb = sb("wv_sb", [P, D])
        wo_sb = sb("wo_sb", [HP * DH, 2, D])
        wr_sb = sb("wr_sb", [P, E])
        bias_sb = sb("bias_sb", [P, D])
        ident = sb("ident", [P, P])
        headmask = sb("headmask", [P, H])
        quadmask = sb("quadmask", [P, 2, HQ])
        window = sb("window", [BLK, 3, P])
        before = sb("before", [P, P], BF16)
        ones = sb("ones", [P, P], BF16)
        erank = sb("erank", [P, E])
        eslot = sb("eslot", [P, E])
        scratch = sb("scratch", [P, 16])
        stats = sb("stats", [P, 4, 6])
        meanvar = sb("meanvar", [P, 4, 2])
        veps = sb("veps", [P, 4])
        rs_i = sb("rs_i", [P, 4], I32)
        rs_a = sb("rs_a", [P, 4])
        rs_y = sb("rs_y", [P, 4])
        xn = sb("xn", [P, 2, D])
        xn2 = sb("xn2", [P, 2, D])
        xn2T = sb("xn2T", [P, 2 * P])
        xnT = sb("xnT", [P, 2 * P])
        qT = sb("qT", [P, 2, 2, 2 * P])
        kT = sb("kT", [P, QUADS, 4 * PAIRS_PER_SEQ + 1, P])
        v_sb = sb("v_sb", [P, 2, 4, HP, VW])
        qbd = [[sb(f"qbd{s}{half}", [P, 2, HQ, BLK]) for half in range(2)] for s in range(2)]
        negmax = sb("negmax", [P, 4, 4])
        probs = sb("probs", [P, 4, 4, P])
        probsT = sb("probsT", [P, 2, 4, P])
        rden = sb("rden", [P, 2, 2 * HP])
        ctx_sb = sb("ctx_sb", [P, 2, 3 * HP, DH])
        ctxT = sb("ctxT", [HP * DH, 2, 2, 2, BLK])
        xbias = sb("xbias", [P, 2, 2, D])
        r_m = sb("r_m", [P, GROUP])
        r_sh = sb("r_sh", [P, GROUP, E])
        r_ex = sb("r_ex", [P, GROUP, E])
        r_t = sb("r_t", [P, GROUP, E])
        r_oh = sb("r_oh", [P, 2, GROUP, E])
        r_sel = sb("r_sel", [P, GROUP + 1, E], BF16)
        r_pos = sb("r_pos", [P, GROUP, E])
        r_cnt = sb("r_cnt", [P, E])
        send_rows = sb("send_rows", [P, GROUP, ROW])
        slot_id = sb("slot_id", [P, 2, GROUP], I32)
        w1_sb = sb("w1_sb", [P, 2, F])
        w2_sb = sb("w2_sb", [P, 2, FC, D])
        with nc.sbuf_tensor("empty_rows", [P, SPP, ROW], F32) as empty_rows:
            pass
        xg = sb("xg", [P, 2, SPP, ROW])
        w1_hl = sb("w1_hl", [P, 2, 2, F], F32R)
        xT_hl = sb("xT_hl", [P, 2, 2, 4 * P], F32R)
        y_sb = sb("y_sb", [P, 2, 4, D])

        with nc.sbuf_tensor("x_sb", [P, FRONT + NTILE + 2 * 3, D], F32) as x_sb:
            pass
        hT = sb("hT", [P, 2, FC, 4 * P])

        bank = [ctx.enter_context(nc.psum_tensor(f"bank{i}", [P, 512], F32)) for i in range(8)]
        scores = bank[0:4]
        pt_ps = bank[4]
        o_ps = bank[5:7]
        misc = bank[7]
        last_rows = rows_sb[:, FRONT + NTILE - GROUP:, :]
        last_normed = rows_sb[:, FRONT + NTILE - 2:, 0:D]
        COUNTS = 256
        CTX_T, ATT = 0, 256

        def ctx_view(s):
            return o_ps[s][:, 0:2 * HP * VW].rearrange("p (j c) -> p j c", c=VW)

        ld_qkv = sem("ld_qkv")
        ld_w = sem("ld_w")
        ld_x = [sem(f"ld_x{i}") for i in range(2)]
        c_pool = sem("c_pool")
        ld_mask = sem("ld_mask")
        c_dve = sem("c_dve")
        dve_chain = sem("dve_chain")
        d_init = sem("d_init")
        s_xn = sem("s_xn")
        s_xn2 = sem("s_xn2")
        s_xnT = sem("s_xnT")
        s_xnT_sb = sem("s_xnT_sb")
        s_qk = sem("s_qk")
        s_q_sb = sem("s_q_sb")
        s_k_sb = sem("s_k_sb")
        s_v = sem("s_v")
        s_v_sb = sem("s_v_sb")
        s_qbd = sem("s_qbd")
        s_scores = sem("s_scores")
        s_max = sem("s_max")
        s_exp = sem("s_exp")
        s_pt = sem("s_pt")
        s_pt_sb = sem("s_pt_sb")
        s_pv = sem("s_pv")
        s_ctx = sem("s_ctx")
        s_ctxT = sem("s_ctxT")
        s_ctxT_sb = sem("s_ctxT_sb")
        s_att = sem("s_att")
        s_x2 = sem("s_x2")
        s_xn2T = sem("s_xn2T")
        s_xn2T_sb = sem("s_xn2T_sb")
        s_lg = sem("s_lg")
        s_lg_sb = sem("s_lg_sb")
        s_rows = sem("s_rows")
        s_xbias = sem("s_xbias")
        s_out = sem("s_out")
        s_shift = sem("s_shift")
        s_rexp = sem("s_rexp")
        s_sel = sem("s_sel")
        s_pos = sem("s_pos")
        s_slot = sem("s_slot")
        s_send = sem("s_send")
        s_turn_sp = sem("s_turn_sp")
        s_turn_pool = sem("s_turn_pool")
        s_turn_dve = sem("s_turn_dve")
        s_scat = sem("s_scat")
        s_sent = sem("s_sent")
        ld_e = [sem(f"ld_e{i}") for i in range(2)]
        ld_g = [[sem(f"ld_g{i}_{c}") for c in range(CHUNKS)] for i in range(2)]
        f_w = sem("f_w")
        f_w_hl = sem("f_w_hl")
        f_xT = sem("f_xT")
        f_xT_hi = sem("f_xT_hi")
        f_xT_lo = sem("f_xT_lo")
        f_h = sem("f_h")
        f_gelu = sem("f_gelu")
        f_y = sem("f_y")
        f_y_sb = sem("f_y_sb")
        f_add = [sem(f"f_add{i}") for i in range(2)]
        f_added = sem("f_added")

        block = ctx.enter_context(nc.Block())

        def walk(engine, pair):
            with engine.Fori(1, PAIRS_PER_SEQ) as n:
                pair(n)
            with engine.Fori(1, BATCH) as b:
                with engine.Fori(0, ROUTED_AT) as i:
                    pair(b * PAIRS_PER_SEQ + i)
                pair(b * PAIRS_PER_SEQ + ROUTED_AT, b - 1)
                pair(b * PAIRS_PER_SEQ + ROUTED_AT + 1)

        @block.sync
        def _(sp):
            xr = x.rearrange("b (s p) d -> p (b s) d", p=P)
            sp.dma_start(x_sb[:, FRONT:FRONT + 16, :], xr[:, 0:16, :]).then_inc(ld_x[0], 16)
            for src, dst in ((wq, wq_sb), (wk, wk_sb), (wv, wv_sb)):
                sp.dma_start(dst[:, :], src).then_inc(ld_qkv, 16)
            sp.dma_start(wr_sb[:, :], w_router).then_inc(ld_w, 16)
            sp.wait_ge(s_xn, 1)
            wo4 = wo.rearrange("(j two d) n -> two j d n", two=2, d=DH)
            for two in range(2):
                for j in range(HP):
                    sp.dma_start(wo_sb[j * DH:(j + 1) * DH, two, :], wo4[two, j]).then_inc(ld_w, 16)
            sp.dma_start(bias_sb[:, :], bias.rearrange("a b d -> (a b) d").to_broadcast([P, D])).then_inc(ld_w, 16)
            sp.dma_start(x_sb[:, FRONT + 16:FRONT + NTILE, :], xr[:, 16:NTILE, :]).then_inc(ld_x[1], 16)
            sp.wait_ge(c_pool, 21)
            for e in range(E):
                sp.dma_start(slots_dram[e * CAP:(e + 1) * CAP, :].rearrange("(p j) w -> p (j w)", p=P),
                             empty_rows[:, :, :].rearrange("p j w -> p (j w)")).then_inc(d_init, 16)
            sp.dma_start(out[T:T + CAP, :].rearrange("(p j) w -> p j w", p=P),
                         empty_rows[:, :, 0:D]).then_inc(d_init, 16)
            out_tiles = out[0:T, :].rearrange("(t p) d -> p t d", p=P)

            def keep_rows(n):
                sp.wait_ge(s_xn2, n + 1)
                sp.dma_start(rows_sb[:, bass.ds(2 * n, 2), 0:D], xn2[:, :, :]).then_inc(s_rows, 16)

            def stage(g, n):
                sp.wait_ge(s_rows, START + 16 * (n + 1))
                sp.sem_inc(s_turn_sp, 1)
                sp.wait_ge(s_slot, g + 1)
                sp.dma_start(send_rows[:, :, :],
                             rows_sb[:, bass.ds(FRONT + g * GROUP, GROUP), :]).then_inc(s_send, 16)

            def put_out(n):
                sp.wait_ge(s_xbias, n + 1)
                sp.dma_start(out_tiles[:, bass.ds(2 * n, 2), :],
                             xbias[:, bass.ds(n % 2, 1)].rearrange("p o s d -> p (o s) d")).then_inc(s_out, 16)

            def pair(n, g=None):
                put_out(n - 1)
                keep_rows(n)
                if g is not None:
                    stage(g, n)

            keep_rows(0)
            walk(sp, pair)
            put_out(NPAIR - 1)
            keep_rows(NPAIR)
            slots_e = slots_dram.rearrange("(e p j) w -> p e (j w)", e=E, p=P)
            w1_e = w1.rearrange("e h f -> h e f")
            w2_e = w2.rearrange("e (c p) h -> p e c h", p=P)

            def load_weights(e, r):
                sp.dma_start(w1_sb[:, r:r + 1, :], w1_e[:, bass.ds(e, 1), :]).then_inc(ld_e[r], 16)
                sp.dma_start(w2_sb[:, r:r + 1, :, :], w2_e[:, bass.ds(e, 1)]).then_inc(ld_e[r], 16)

            def load_slots(e, r):
                for c in range(CHUNKS):
                    sp.dma_start(xg[:, r:r + 1, 4 * c:4 * c + 4, :].rearrange("p o j w -> p o (j w)"),
                                 slots_e[:, bass.ds(e, 1), 4 * c * ROW:4 * (c + 1) * ROW]).then_inc(ld_g[r][c], 16)

            load_weights(0, 0)
            load_weights(1, 1)
            sp.wait_ge(s_out, START + 16 * NPAIR)
            sp.wait_ge(d_init, 16 * (E + 1))
            sp.wait_ge(s_scat, 16 * TOPK * NTILE)
            load_slots(0, 0)
            load_slots(1, 1)
            with sp.Fori(1, E // 2) as ee:
                for r in range(2):
                    sp.wait_ge(f_y, CHUNKS * (2 * ee - 1 + r))
                    sp.sem_inc(s_turn_sp, 1)
                    load_weights(2 * ee + r, r)
                    for i in range(2):
                        sp.wait_ge(f_add[i], ADDED * (2 * ee - 1 + r))
                        sp.sem_inc(s_turn_sp, 1)
                    load_slots(2 * ee + r, r)

        @block.gpsimd
        def _(pool):
            pool.memset(ident[:, :], 0.0).then_inc(c_pool, 1)
            pool.memset(headmask[:, :], 1.0).then_inc(c_pool, 1)
            pool.memset(window[:, :, :], 0.0).then_inc(c_pool, 1)
            pool.memset(before[:, :], 1.0).then_inc(c_pool, 1)
            pool.wait_ge(c_pool, 4)
            pool.affine_select(out=ident[:, :], in_=ident[:, :], compare_op=ALU.not_equal, fill=1.0, base=0,
                               pattern=[[-1, P]], channel_multiplier=1).then_inc(c_pool, 1)
            pool.affine_select(out=headmask[:, :], in_=headmask[:, :], compare_op=ALU.is_ge, fill=0.0, base=0,
                               pattern=[[-DH, H]], channel_multiplier=1).then_inc(c_pool, 1)
            pool.affine_select(out=before[:, :], in_=before[:, :], compare_op=ALU.is_gt, fill=0.0, base=0,
                               pattern=[[1, P]], channel_multiplier=-1).then_inc(c_pool, 1)
            pool.wait_ge(c_pool, 7)
            pool.affine_select(out=headmask[:, :], in_=headmask[:, :], compare_op=ALU.is_ge, fill=0.0,
                               base=DH - 1, pattern=[[DH, H]], channel_multiplier=-1).then_inc(c_pool, 1)
            for w, blk in enumerate((0, 1, 0)):
                own, other = slice(blk * BLK, blk * BLK + BLK), slice((1 - blk) * BLK, (1 - blk) * BLK + BLK)
                pool.affine_select(out=window[:, w, own], in_=window[:, w, own], compare_op=ALU.is_ge,
                                   fill=NEG, base=0, pattern=[[-1, BLK]], channel_multiplier=1).then_inc(c_pool, 1)
                pool.affine_select(out=window[:, w, other], in_=window[:, w, other], compare_op=ALU.is_gt,
                                   fill=NEG, base=0, pattern=[[1, BLK]], channel_multiplier=-1).then_inc(c_pool, 1)
            pool.wait_ge(c_pool, 14)
            pool.memset(window[:, 2, BLK:], NEG).then_inc(c_pool, 1)
            pool.memset(kT[:, 0:2, :, :], 0.0).then_inc(c_pool, 1)

            def late_constants():
                pool.memset(empty_rows[:, :, :], 0.0).then_inc(c_pool, 1)
                pool.iota(rows_sb[:, FRONT:FRONT + NTILE, ROW - 1].bitcast(I32), pattern=[[P, NTILE]], base=0,
                          channel_multiplier=1).then_inc(c_pool, 1)
                pool.iota(erank[:, :], pattern=[[-1, E]], base=E, channel_multiplier=0,
                          allow_small_or_imprecise_dtypes=True).then_inc(c_pool, 1)
                pool.iota(eslot[:, :], pattern=[[CAP, E]], base=0, channel_multiplier=0,
                          allow_small_or_imprecise_dtypes=True).then_inc(c_pool, 1)
                pool.wait_ge(c_pool, 20)
                pool.iota(empty_rows[:, :, ROW - 1].bitcast(I32), pattern=[[1, SPP]], base=T,
                          channel_multiplier=SPP).then_inc(c_pool, 1)

            def spread_queries(m, s):
                for half in range(2):
                    q = qT[:, half, bass.ds(m % 2, 1), s * P:(s + 1) * P].rearrange("p o (b q) -> p (o b) q", b=2)
                    heads = quadmask[:, half, :].unsqueeze(1).unsqueeze(3)
                    last = pool.tensor_tensor(out=qbd[s][half][:, :, :, :],
                                              in0=q.unsqueeze(2).to_broadcast([P, 2, HQ, BLK]),
                                              in1=heads.to_broadcast([P, 2, HQ, BLK]), op=ALU.mult)
                last.then_inc(s_qbd, 1)

            def send(rows, tiles):
                for j in tiles:
                    for k in range(2):
                        pool.indirect_dma_start(
                            out=slots_dram,
                            out_offset=bass.IndirectOffsetOnAxis(ap=slot_id[:, k, j:j + 1].bitcast(U32), axis=0),
                            in_=rows[:, j, :],
                            in_offset=None, bounds_check=E * CAP - 1, oob_is_err=False).then_inc(s_scat, 16)

            def pair(n, g=None):
                pool.wait_ge(s_q_sb, n + 2)
                pool.wait_ge(s_scores, UNITS * n + 4)
                spread_queries(n + 1, 0)
                if g is not None:
                    pool.wait_ge(s_send, 16 * g + 16)
                    pool.sem_inc(s_turn_pool, 1)
                    send(send_rows, range(GROUP // 2))
                pool.wait_ge(s_scores, UNITS * n + 8)
                spread_queries(n + 1, 1)

            def leave(n):
                pool.wait_ge(s_x2, START + 2 * n + 2)
                pool.wait_ge(s_out, START + 16 * n)
                pool.tensor_tensor(out=xbias[:, bass.ds(n % 2, 1)].rearrange("p o s d -> p (o s) d"),
                                   in0=x_sb[:, bass.ds(2 * n + FRONT, 2), :],
                                   in1=bias_sb[:, :].unsqueeze(1).to_broadcast([P, 2, D]),
                                   op=ALU.add).then_inc(s_xbias, 1)

            pool.wait_ge(c_dve, 1)
            pool.wait_ge(s_q_sb, 1)
            spread_queries(0, 0)
            spread_queries(0, 1)
            late_constants()
            pool.wait_ge(ld_w, 16 * 18)
            pair(0)
            with pool.Fori(1, PAIRS_PER_SEQ) as n:
                pair(n)
                leave(n - 1)
            pool.wait_ge(d_init, 16 * (E + 1))
            with pool.Fori(1, BATCH) as b:
                for i in range(PAIRS_PER_SEQ):
                    n = b * PAIRS_PER_SEQ + i
                    pair(n, b - 1 if i == ROUTED_AT + 1 else None)
                    leave(n - 1)
                send(send_rows, range(GROUP // 2, GROUP))
                pool.wait_ge(s_scat, 16 * TOPK * GROUP * b)
                pool.sem_inc(s_sent, 1)
            leave(NPAIR - 1)
            pool.wait_ge(s_slot, NGROUP)
            pool.wait_ge(s_rows, START + 16 * (NPAIR + 1))
            send(last_rows, range(GROUP))

            def add_results(ee, r):
                for c in range(CHUNKS):
                    pool.wait_ge(f_y_sb, 2 + (2 * ee + r) * CHUNKS + c + 1)
                    pool.sem_inc(s_turn_pool, 1)
                    pool.wait_ge(d_init, 16 * (E + 1))
                    for k in range(4):
                        pool.indirect_dma_start(
                            out=out,
                            out_offset=bass.IndirectOffsetOnAxis(
                                ap=xg[:, r, 4 * c + k, ROW - 1:ROW].bitcast(U32), axis=0),
                            in_=y_sb[:, c % 2, k, :],
                            in_offset=None, bounds_check=T + CAP - 1, oob_is_err=True,
                            compute_op=ALU.add).then_inc(f_add[c % 2], 16)
                pool.wait_ge(f_add[0], ADDED * (2 * ee + r + 1))
                pool.sem_inc(s_turn_pool, 1)
                pool.wait_ge(f_add[1], ADDED * (2 * ee + r + 1))
                pool.sem_inc(f_added, 1)

            pool.wait_ge(s_out, START + 16 * NPAIR)
            with pool.Fori(0, E // 2) as ee:
                for r in range(2):
                    add_results(ee, r)

        @block.scalar
        def _(act):
            act.wait_ge(c_pool, 15)
            for g in (2, 3, 0, 1):
                if g == 0:
                    act.wait_ge(c_pool, 16)
                other = slice(BLK, P) if g < QUADS // 2 else slice(0, BLK)
                of_pairs = kT[other, g, 0:4 * PAIRS_PER_SEQ, :].rearrange("p (i b) j -> p i b j", b=2)
                for blk in range(2):
                    act.dma_start(of_pairs[:, 1 - blk:, blk, :],
                                  window[:, blk:blk + 1, :].to_broadcast([BLK, 2 * PAIRS_PER_SEQ - (1 - blk), P])
                                  ).then_inc(ld_mask, 16)
                act.dma_start(kT[other, g, 0, :], window[:, 2, :]).then_inc(ld_mask, 16)

            def query_key(m):
                act.wait_ge(s_qk, m + 1)
                for half in range(2):
                    f = slice(half * P // 2, (half + 1) * P // 2)
                    last = nc.scalar.activation(qT[f, half, bass.ds(m % 2, 1), :].rearrange("p o q -> p (o q)"),
                                                misc[f, 0:2 * P], ACT.Copy, scale=float(DH) ** -0.5)
                last.then_inc(s_q_sb, 1)

            def keys(m, quads):
                for g in quads:
                    q = slice(32 * g, 32 * g + 32)
                    blocks = misc[q, 2 * P:4 * P].rearrange("p (t b j) -> p t b j", t=2, b=2)
                    for odd in range(2):
                        windows = kT[q, g, bass.ds(m % PAIRS_PER_SEQ * 4 + odd, 4), odd * BLK:odd * BLK + BLK]
                        last = nc.scalar.copy(windows.rearrange("p (t w) j -> p t w j", t=2),
                                              blocks[:, :, odd, :].unsqueeze(2).to_broadcast([32, 2, 2, BLK]))
                last.then_inc(s_k_sb, 1)

            def prep_T(m):
                act.wait_ge(s_xnT, m + 1)
                nc.scalar.copy(xnT[:, :], misc[:, 0:2 * P]).then_inc(s_xnT_sb, 1)

            def values(m):
                act.wait_ge(s_v, m + 1)
                low, high = slice(0, BLK), slice(BLK, P)

                def put(half, ring, windows, t):
                    v = v_sb[half, bass.ds(ring, 1), windows, :, 0:2 * DH].rearrange("p o w j c -> p (o w) j c")
                    tile = misc[half, t * P:(t + 1) * P].rearrange("p (j c) -> p j c", j=HP).unsqueeze(1)
                    return nc.scalar.activation(v, tile.to_broadcast([BLK, windows.stop - windows.start, HP, 2 * DH]),
                                                ACT.Copy)

                put(low, m % 2, slice(0, 2), 0)
                put(low, m % 2, slice(2, 4), 1)
                put(high, m % 2, slice(1, 3), 0)
                put(high, m % 2, slice(3, 4), 1)
                put(high, (m + 1) % 2, slice(0, 1), 1).then_inc(s_v_sb, 1)

            def exps(n, k):
                act.wait_ge(s_max, UNITS * n + k + 1)
                for c in range(4):
                    last = nc.scalar.activation(probs[:, k % 4, c, :], scores[k % 4][:, c * P:(c + 1) * P], ACT.Exp,
                                                bias=negmax[:, k % 4, c:c + 1])
                last.then_inc(s_exp, 1)

            def probs_T(n, k):
                act.wait_ge(s_pt, UNITS * n + k + 1)
                nc.scalar.copy(probsT[:, k % 2, :, :].rearrange("p c j -> p (c j)"), pt_ps[:, :]).then_inc(s_pt_sb, 1)

            def context_T(n, s):
                act.wait_ge(s_ctxT, 2 * n + s + 1)
                nc.scalar.activation(ctxT[:, s, :, :, :],
                                     o_ps[s][0:HP * DH, CTX_T:CTX_T + 2 * P].rearrange(
                                         "p (b h q) -> p h b q", b=2, h=2), ACT.Copy).then_inc(s_ctxT_sb, 1)

            def router_T(n):
                act.wait_ge(s_xn2T, START + n + 1)
                nc.scalar.activation(xn2T[:, :], misc[:, 0:2 * P], ACT.Copy).then_inc(s_xn2T_sb, 1)

            def gate_exps(g):
                act.wait_ge(s_shift, g + 1)
                nc.scalar.activation(r_ex[:, :, :], r_sh[:, :, :], ACT.Exp).then_inc(s_rexp, 1)

            def pair(n, g=None, first=False):
                for k in range(UNITS):
                    if k in BY_ACT:
                        probs_T(n, k)
                    if k + LEAD < UNITS:
                        exps(n, k + LEAD)
                    else:
                        exps(n + 1, k + LEAD - UNITS)
                    if k == 1 and not first:
                        context_T(n - 1, 1)
                    if k == 0:
                        prep_T(n + 1)
                    if k == 1:
                        query_key(n + 1)
                        keys(n + 1, (0, 1))
                    if k == 2:
                        keys(n + 1, (2, 3))
                    if k == 3:
                        values(n + 1)
                    if k == 3 and g is not None:
                        gate_exps(g)
                    if k == 5:
                        router_T(n)
                    if k == 6:
                        context_T(n, 0)

            prep_T(0)
            query_key(0)
            keys(0, (0, 1))
            keys(0, (2, 3))
            values(0)
            for k in range(LEAD):
                exps(0, k)
            pair(0, first=True)
            walk(act, pair)
            context_T(NPAIR - 1, 1)
            router_T(NPAIR)
            router_T(NPAIR + 1)
            gate_exps(NGROUP - 1)

            def slots_hi(q, c):
                act.wait_ge(f_xT, q + 1)
                nc.scalar.activation(xT_hl[:, c % 2, 0, :], pt_ps[:, :], ACT.Copy).then_inc(f_xT_hi, 1)

            def experts(ee, last=False):
                for c in range(2 * CHUNKS):
                    q = ee * 2 * CHUNKS + c
                    for f in range(FC):
                        act.wait_ge(f_h, q * FC + f + 1)
                        nc.scalar.activation(hT[:, c % 2, f, :], bank[f][:, :], ACT.Gelu_apprx_tanh).then_inc(f_gelu, 1)
                    if not (last and c == 2 * CHUNKS - 1):
                        slots_hi(q + 1, c + 1)

            slots_hi(0, 0)
            with act.Fori(0, E // 2 - 1) as ee:
                experts(ee)
            experts(E // 2 - 1, last=True)

        @block.vector
        def _(dve):
            class Chain:
                def __init__(self, base):
                    self.base, self.steps = base, 0

                def mark(self, instruction):
                    instruction.then_inc(dve_chain, 1)
                    self.steps += 1

                def wait(self):
                    dve.wait_ge(dve_chain, self.base + self.steps)

            def norms(chain, first, second, steps, normed=xn2):
                tiles = [x_sb[:, bass.ds(2 * a + FRONT + s, 1), :].rearrange("p o d -> p (o d)")
                         for a in (first, second) if a is not None for s in range(2)]
                w = len(tiles)
                v, y, a = veps[:, 0:w], rs_y[:, 0:w], rs_a[:, 0:w]
                mean, diff = meanvar[:, 0:w, 0], meanvar[:, 0:w, 1]
                for step in steps:
                    if step > 0:
                        chain.wait()
                    if step == 0:
                        for i, t in enumerate(tiles):
                            last = nc.vector.bn_stats(stats[:, i, :], t)
                        chain.mark(last)
                    elif step == 1:
                        nc.vector.tensor_tensor(out=mean, in0=stats[:, 0:w, 1], in1=stats[:, 0:w, 4], op=ALU.add)
                        nc.vector.tensor_tensor(out=v, in0=stats[:, 0:w, 2], in1=stats[:, 0:w, 5], op=ALU.add)
                        chain.mark(nc.vector.tensor_tensor(out=diff, in0=stats[:, 0:w, 1], in1=stats[:, 0:w, 4],
                                                           op=ALU.subtract))
                    elif step == 2:
                        nc.vector.tensor_scalar(mean, mean, 0.5, None, ALU.mult)
                        nc.vector.tensor_scalar(v, v, 1.0 / D, EPS, ALU.mult, ALU.add)
                        chain.mark(nc.vector.scalar_tensor_tensor(out=diff, in0=diff, scalar=0.25, in1=diff,
                                                                  op0=ALU.mult, op1=ALU.mult))
                    elif step == 3:
                        chain.mark(nc.vector.tensor_tensor(out=v, in0=v, in1=diff, op=ALU.add))
                    elif step == 4:
                        chain.mark(nc.vector.tensor_scalar(rs_i[:, 0:w], v.bitcast(I32), 1, None,
                                                           ALU.logical_shift_right))
                    elif step == 5:
                        chain.mark(nc.vector.tensor_scalar(y.bitcast(I32), rs_i[:, 0:w], -1.0, MAGIC, ALU.mult, ALU.add))
                    elif step < 15 and step % 3 == 0:
                        chain.mark(nc.vector.scalar_tensor_tensor(out=a, in0=y, scalar=-0.5, in1=y,
                                                                  op0=ALU.mult, op1=ALU.mult))
                    elif step < 15 and step % 3 == 1:
                        chain.mark(nc.vector.tensor_tensor(out=a, in0=a, in1=v, op=ALU.mult))
                    elif step < 15:
                        chain.mark(nc.vector.scalar_tensor_tensor(out=y, in0=a, scalar=1.5, in1=y,
                                                                  op0=ALU.add, op1=ALU.mult))
                    else:
                        i = 0
                        for which, dst, done in ((first, xn, s_xn), (second, normed, s_xn2)):
                            if which is None:
                                continue
                            for s in range(2):
                                last = nc.vector.tensor_scalar(dst[:, s, :], tiles[i], meanvar[:, i, 0:1],
                                                               rs_y[:, i:i + 1], ALU.subtract, ALU.mult)
                                i += 1
                            last.then_inc(done, 1)

            ALL = range(16)

            def score_max(n, k):
                dve.wait_ge(s_scores, UNITS * n + k + 1)
                nc.vector.tensor_reduce(negmax[:, k % 4, :], scores[k % 4][:, :].rearrange("p (c j) -> p c j", c=4),
                                        AX.X, ALU.max, negate=True).then_inc(s_max, 1)

            def probs_T(n, k):
                dve.wait_ge(s_pt, UNITS * n + k + 1)
                nc.vector.tensor_copy(probsT[:, k % 2, :, :].rearrange("p c j -> p (c j)"),
                                      pt_ps[:, :]).then_inc(s_pt_sb, 1)

            def normalise(chain, n, s):
                dve.wait_ge(s_pv, UNITS * n + 4 * s + 4)
                o = ctx_view(s)
                chain.mark(nc.vector.reciprocal(rden[:, s, :], o[:, :, 2 * DH]))
                chain.wait()
                for par in range(2):
                    q = slice(par * BLK, (par + 1) * BLK)
                    last = nc.vector.tensor_tensor(out=ctx_sb[q, s, 0:2 * HP, :], in0=o[q, :, par * DH:(par + 1) * DH],
                                                   in1=rden[q, s, :].unsqueeze(2).to_broadcast([BLK, 2 * HP, DH]),
                                                   op=ALU.mult)
                last.then_inc(s_ctx, 1)

            def residual(n, s):
                dve.wait_ge(s_att, 2 * n + s + 1)
                t = x_sb[:, bass.ds(2 * n + FRONT + s, 1), :].rearrange("p o d -> p (o d)")
                nc.vector.tensor_tensor(out=t, in0=o_ps[s][:, ATT:ATT + D], in1=t, op=ALU.add).then_inc(s_x2, 1)

            def logits(n):
                dve.wait_ge(s_lg, n + 1)
                nc.vector.tensor_copy(logits_sb[:, bass.ds(2 * n, 2), :].rearrange("p t e -> p (t e)"),
                                      misc[:, 0:2 * E]).then_inc(s_lg_sb, 1)

            def pick(chain, k, part):
                rank = erank[:, :].unsqueeze(1).to_broadcast([P, GROUP, E])
                over_e = r_m[:, :].unsqueeze(2).to_broadcast([P, GROUP, E])
                chain.wait()
                if part == "others":
                    chain.mark(nc.vector.scalar_tensor_tensor(out=r_pos[:, :, :], in0=r_oh[:, 0, :, :], scalar=-1.0e9,
                                                              in1=r_sh[:, :, :], op0=ALU.mult, op1=ALU.add))
                elif part == "largest":
                    chain.mark(nc.vector.tensor_reduce(r_m[:, :], r_pos[:, :, :], AX.X, ALU.max))
                elif part == "equal":
                    if k == 0:
                        chain.mark(nc.vector.tensor_scalar(r_t[:, :, :], r_sh[:, :, :], 0.0, None, ALU.is_equal))
                    else:
                        chain.mark(nc.vector.tensor_tensor(out=r_t[:, :, :], in0=r_pos[:, :, :], in1=over_e,
                                                           op=ALU.is_equal))
                elif part == "ranks":
                    chain.mark(nc.vector.tensor_tensor(out=r_t[:, :, :], in0=r_t[:, :, :], in1=rank, op=ALU.mult))
                elif part == "first":
                    chain.mark(nc.vector.tensor_reduce(r_m[:, :], r_t[:, :, :], AX.X, ALU.max))
                else:
                    chain.mark(nc.vector.tensor_tensor(out=r_oh[:, k, :, :], in0=rank, in1=over_e, op=ALU.is_equal))

            def shift(chain, g, part):
                lg = logits_sb[:, bass.ds(FRONT + g * GROUP, GROUP), :]
                if part == 0:
                    chain.mark(nc.vector.tensor_reduce(r_m[:, :], lg, AX.X, ALU.max))
                elif part == 1:
                    chain.wait()
                    chain.mark(nc.vector.tensor_tensor(out=r_sh[:, :, :], in0=lg,
                                                       in1=r_m[:, :].unsqueeze(2).to_broadcast([P, GROUP, E]),
                                                       op=ALU.subtract))
                else:
                    chain.wait()
                    nc.vector.tensor_scalar(r_sh[:, :, :], r_sh[:, :, :], LOWEST, None, ALU.max).then_inc(s_shift, 1)
                    dve.wait_ge(s_shift, g + 1)

            def gates(chain, g, part):
                if part == 0:
                    chain.wait()
                    nc.vector.tensor_tensor(out=r_sel[:, 0:GROUP, :], in0=r_oh[:, 0, :, :], in1=r_oh[:, 1, :, :],
                                            op=ALU.add).then_inc(s_sel, 1)
                    dve.wait_ge(s_rexp, g + 1)
                    chain.mark(nc.vector.tensor_reduce(r_m[:, :], r_ex[:, :, :], AX.X, ALU.add))
                elif part == 1:
                    chain.wait()
                    chain.mark(nc.vector.reciprocal(r_m[:, :], r_m[:, :]))
                else:
                    chain.wait()
                    nc.vector.tensor_tensor(out=rows_sb[:, bass.ds(FRONT + g * GROUP, GROUP), D:D + E], in0=r_ex[:, :, :],
                                            in1=r_m[:, :].unsqueeze(2).to_broadcast([P, GROUP, E]), op=ALU.mult)

            def positions(chain, g, part):
                if part == 0:
                    dve.wait_ge(s_pos, g + 1)
                    pos = misc[:, COUNTS:COUNTS + (GROUP + 1) * E].rearrange("p (t e) -> p t e", e=E)
                    chain.mark(nc.vector.tensor_tensor(out=r_pos[:, :, :], in0=pos[:, 0:GROUP, :],
                                                       in1=r_cnt[:, :].unsqueeze(1).to_broadcast([P, GROUP, E]),
                                                       op=ALU.add))
                    chain.wait()
                    chain.mark(nc.vector.tensor_tensor(out=r_cnt[:, :], in0=pos[:, GROUP, :], in1=r_cnt[:, :],
                                                       op=ALU.add))
                    return
                chain.wait()
                if part == 1:
                    chain.mark(nc.vector.tensor_scalar(r_t[:, :, :], r_pos[:, :, :], float(CAP), float(1 << 20),
                                                       ALU.is_ge, ALU.mult))
                elif part == 2:
                    chain.mark(nc.vector.tensor_tensor(out=r_pos[:, :, :], in0=r_pos[:, :, :], in1=r_t[:, :, :], op=ALU.add))
                elif part == 3:
                    chain.mark(nc.vector.tensor_tensor(out=r_pos[:, :, :], in0=r_pos[:, :, :],
                                                       in1=eslot[:, :].unsqueeze(1).to_broadcast([P, GROUP, E]), op=ALU.add))
                elif part == 4:
                    for k in range(2):
                        last = nc.vector.tensor_tensor(out=r_oh[:, k, :, :], in0=r_oh[:, k, :, :], in1=r_pos[:, :, :],
                                                       op=ALU.mult)
                    chain.mark(last)
                else:
                    dve.wait_ge(s_sent, START + g)
                    for k in range(2):
                        last = nc.vector.tensor_reduce(slot_id[:, k, :], r_oh[:, k, :, :], AX.X, ALU.max)
                    last.then_inc(s_slot, 1)

            def route(chain, g, at):
                if at == 0:
                    for part in range(3):
                        shift(chain, g, part)
                elif at == 1:
                    for part in ("equal", "ranks", "first", "mark"):
                        pick(chain, 0, part)
                elif at == 2:
                    for part in ("others", "largest", "equal"):
                        pick(chain, 1, part)
                elif at == 3:
                    for part in ("ranks", "first", "mark"):
                        pick(chain, 1, part)
                elif at == 4:
                    for part in range(3):
                        gates(chain, g, part)
                elif at == 7:
                    for part in range(6):
                        positions(chain, g, part)

            nc.vector.memset(kT[96:128, 2, :, :], 0.0)
            nc.vector.memset(kT[64:96, 3, :, :], 0.0)
            nc.vector.memset(kT[64:96, 2, 0, :], 0.0)
            nc.vector.memset(kT[96:128, 3, 0, :], 0.0)
            for i, free in enumerate((s_x2, s_xn2T, s_lg_sb, s_pt_sb, s_rows, s_out, s_sent, f_added)):
                nc.vector.memset(scratch[:, i:i + 1], 0.0).then_inc(free, START)
            nc.vector.memset(scratch[:, 15:16], 0.0).then_inc(f_y_sb, 2)

            chain = Chain(0)
            dve.wait_ge(ld_x[0], 16)
            norms(chain, 0, None, ALL)
            dve.wait_ge(c_pool, 8)
            for half in range(2):
                f, other = (slice(h * BLK, (h + 1) * BLK) for h in (half, 1 - half))
                nc.vector.tensor_reduce(quadmask[f, half, :], headmask[f, :].rearrange("p (g h) -> p h g", g=QUADS),
                                        AX.X, ALU.add)
                nc.vector.memset(quadmask[other, half, :], 1.0)
                one_hot = ident[other, other].unsqueeze(1).to_broadcast([BLK, 8, BLK])
                last = nc.vector.tensor_copy(qT[other, half, :, :].rearrange("p r (b q) -> p (r b) q", q=BLK), one_hot)
            last.then_inc(c_dve, 1)
            nc.vector.memset(x_sb[:, 0:FRONT, :], 0.0)
            nc.vector.memset(x_sb[:, FRONT + NTILE:, :], 0.0)
            nc.vector.memset(ones[:, :], 1.0)
            nc.vector.memset(ctx_sb[:, :, 2 * HP:, :], 0.0)
            nc.vector.memset(v_sb[:, :, :, :, 2 * DH:], 1.0)
            nc.vector.memset(v_sb[BLK:, 0, 0, :, 0:2 * DH], 0.0)
            nc.vector.memset(r_sel[:, GROUP, :], 0.0)
            nc.vector.memset(r_cnt[:, :], 0.0).then_inc(c_dve, 1)
            dve.wait_ge(c_dve, 2)
            dve.wait_ge(s_xnT, 1)
            norms(chain, 1, None, ALL)
            for k in range(LEAD):
                score_max(0, k)
            norms(chain, 2, -2, range(8))
            PRE = chain.steps - 1
            PER, ROUTE_STEPS = 15 + 2, 2 + 10 + 2 + 6

            def norm_step(chain, n, slot):
                if slot >= 8:
                    norms(chain, n + 3, n - 1, (slot - 8,))
                else:
                    norms(chain, n + 2, n - 2, (slot + 8,))

            def pair(n, g=None, first=False):
                chain = Chain(n * PER + PRE + ROUTE_STEPS * pair.routed + (1 if first else 0))
                for k in range(UNITS):
                    if k not in BY_ACT:
                        probs_T(n, k)
                    if k == 4:
                        dve.wait_ge(s_x2, START + 2 * n)
                    norm_step(chain, n, 2 * k)
                    if k + LEAD < UNITS:
                        score_max(n, k + LEAD)
                    else:
                        score_max(n + 1, k + LEAD - UNITS)
                    if k == 3:
                        dve.wait_ge(s_xn2T, START + n)
                        dve.wait_ge(s_rows, START + 16 * n)
                        dve.wait_ge(s_xnT, n + 2)
                    norm_step(chain, n, 2 * k + 1)
                    if k == 0 and not first:
                        normalise(chain, n - 1, 1)
                    if k == 3 and not first:
                        residual(n - 1, 1)
                    if k == 5:
                        normalise(chain, n, 0)
                    if g is not None:
                        route(chain, g, k)
                    if k == 7:
                        logits(n)
                        residual(n, 0)
                assert chain.steps == (PER if not first else PER - 1) + (0 if g is None else ROUTE_STEPS)

            pair.routed = 0
            pair(0, first=True)
            pair(1)
            dve.wait_ge(ld_x[1], 16)
            dve.wait_ge(c_pool, 21)
            with dve.Fori(2, PAIRS_PER_SEQ) as n:
                pair(n)
            with dve.Fori(1, BATCH) as b:
                pair.routed = b - 1
                with dve.Fori(0, ROUTED_AT) as i:
                    pair(b * PAIRS_PER_SEQ + i)
                pair(b * PAIRS_PER_SEQ + ROUTED_AT, b - 1)
                pair.routed = b
                pair(b * PAIRS_PER_SEQ + ROUTED_AT + 1)
            chain = Chain(NPAIR * PER + PRE + ROUTE_STEPS * (BATCH - 1))
            normalise(chain, NPAIR - 1, 1)
            dve.wait_ge(s_xn2T, START + NPAIR)
            dve.wait_ge(s_rows, START + 16 * NPAIR)
            dve.wait_ge(s_xnT, NPAIR + 1)
            norms(chain, NPAIR + 2, NPAIR - 2, range(8, 16))
            residual(NPAIR - 1, 1)
            dve.wait_ge(s_x2, START + 2 * NPAIR)
            norms(chain, None, NPAIR - 1, range(8))
            logits(NPAIR)
            norms(chain, None, NPAIR - 1, range(8, 16), last_normed)
            logits(NPAIR + 1)
            dve.wait_ge(s_lg_sb, START + NPAIR + 2)
            for k in range(UNITS):
                route(chain, NGROUP - 1, k)

            def split_weights(e, r):
                dve.wait_ge(ld_e[r], 16 * (e - r) + 32)
                dve.sem_inc(s_turn_dve, 1)
                nc.vector.tensor_copy(w1_hl[:, r, 0, :], w1_sb[:, r, :]).then_inc(f_w, 1)
                dve.wait_ge(f_w, e + 1)
                nc.vector.tensor_tensor(out=w1_hl[:, r, 1, :], in0=w1_sb[:, r, :], in1=w1_hl[:, r, 0, :],
                                        op=ALU.subtract).then_inc(f_w_hl, 1)

            def slots_lo(q, c):
                dve.wait_ge(f_xT_hi, q + 1)
                nc.vector.tensor_tensor(out=xT_hl[:, c % 2, 1, :], in0=pt_ps[:, :], in1=xT_hl[:, c % 2, 0, :],
                                        op=ALU.subtract).then_inc(f_xT_lo, 1)

            def gated(ee, q, c):
                r = c // CHUNKS
                dve.wait_ge(f_y, q + 1)
                if c < 2:
                    dve.wait_ge(f_added, START + 2 * ee)
                else:
                    dve.wait_ge(f_add[c % 2], 16 * 4 * (ee * CHUNKS + c // 2))
                gate = xg[:, r, (c % CHUNKS) * 4:(c % CHUNKS) * 4 + 4, bass.ds(D + 2 * ee + r, 1)]
                nc.vector.tensor_tensor(out=y_sb[:, c % 2, :, :],
                                        in0=o_ps[c % 2][:, :].rearrange("p (k d) -> p k d", k=4),
                                        in1=gate.to_broadcast([P, 4, D]), op=ALU.mult).then_inc(f_y_sb, 1)

            def experts(ee, last=False, first=False):
                for c in range(2 * CHUNKS):
                    q = ee * 2 * CHUNKS + c
                    if not (last and c == 2 * CHUNKS - 1):
                        slots_lo(q + 1, c + 1)
                    if c == 1:
                        split_weights(2 * ee + 1, 1)
                    if c == 7 and not last:
                        split_weights(2 * ee + 2, 0)
                    if c > 0:
                        gated(ee, q - 1, c - 1)
                    elif not first:
                        gated(ee - 1, q - 1, 2 * CHUNKS - 1)
                if last:
                    gated(ee, ee * 2 * CHUNKS + 2 * CHUNKS - 1, 2 * CHUNKS - 1)

            split_weights(0, 0)
            slots_lo(0, 0)
            experts(0, first=True)
            with dve.Fori(1, E // 2 - 1) as ee:
                experts(ee)
            experts(E // 2 - 1, last=True)

        @block.tensor
        def _(pe):
            mm = nc.tensor.matmul

            def prep_T(m):
                pe.wait_ge(s_xn, m + 1)
                for s in range(2):
                    last = nc.tensor.transpose(misc[:, s * P:(s + 1) * P], xn[:, s, :], ident[:, :])
                last.then_inc(s_xnT, 1)

            def query_key(m):
                pe.wait_ge(s_xnT_sb, m + 1)
                mm(misc[:, 0:2 * P], wq_sb[:, :], xnT[:, :], start=True, stop=True)
                mm(misc[:, 2 * P:4 * P], wk_sb[:, :], xnT[:, :], start=True, stop=True).then_inc(s_qk, 1)

            def values(m):
                pe.wait_ge(s_k_sb, 2 * (m + 1))
                for t in range(2):
                    last = mm(misc[:, t * P:(t + 1) * P], xnT[:, t * P:(t + 1) * P], wv_sb[:, :], start=True, stop=True)
                last.then_inc(s_v, 1)

            def score(m, k):
                s, blk, half = k // 4, (k // 2) % 2, k % 2
                if k % 4 == 0:
                    pe.wait_ge(s_qbd, 2 * m + s + 1)
                if k == 0:
                    pe.wait_ge(s_k_sb, 2 * (m + 1))
                for c in range(4):
                    j = 4 * half + c
                    h = 2 * j % HQ
                    keys = kT[:, 2 * j // HQ, bass.ds(m % PAIRS_PER_SEQ * 4 + 2 * s + blk, 1), :]
                    last = mm(scores[k % 4][:, c * P:(c + 1) * P],
                              qbd[s][half][:, blk, h:h + 2, :].rearrange("p h q -> p (h q)"),
                              keys.rearrange("p o j -> p (o j)"), start=True, stop=True)
                last.then_inc(s_scores, 1)

            def probs_T(n, k):
                pe.wait_ge(s_exp, UNITS * n + k + 1)
                pe.wait_ge(s_pt_sb, START + UNITS * n + k)
                for c in range(4):
                    last = nc.tensor.transpose(pt_ps[:, c * P:(c + 1) * P], probs[:, k % 4, c, :], ident[:, :])
                last.then_inc(s_pt, 1)

            def weighted(n, k):
                s, blk, half = k // 4, (k // 2) % 2, k % 2
                pe.wait_ge(s_pt_sb, START + UNITS * n + k + 1)
                if k == 0:
                    pe.wait_ge(s_v_sb, n + 1)
                if k % 4 == 0:
                    pe.wait_ge(s_x2, START + 2 * n - 1 + s)
                for c in range(4):
                    j = 4 * half + c
                    v = v_sb[:, bass.ds(n % 2, 1), 2 * s + blk, j, 0:2 * DH + 1].rearrange("p o c -> p (o c)")
                    last = mm(ctx_view(s)[:, blk * HP + j, 0:2 * DH + 1], probsT[:, k % 2, c, :], v, start=True, stop=True)
                last.then_inc(s_pv, 1)

            def context_T(n, s):
                pe.wait_ge(s_ctx, 2 * n + s + 1)
                for blk in range(2):
                    last = nc.tensor.transpose(o_ps[s][:, CTX_T + blk * P:CTX_T + (blk + 1) * P],
                                               ctx_sb[:, s, blk * HP:(blk + 2) * HP, :].rearrange("p j d -> p (j d)"),
                                               ident[:, :])
                last.then_inc(s_ctxT, 1)

            def project(n, s):
                pe.wait_ge(s_ctxT_sb, 2 * n + s + 1)
                for par in range(2):
                    last = mm(o_ps[s][:, ATT:ATT + D], ctxT[:, s, par, :, :].rearrange("p b q -> p (b q)"),
                              wo_sb[:, par, :], start=(par == 0), stop=(par == 1))
                last.then_inc(s_att, 1)

            def router_T(n, normed=xn2):
                pe.wait_ge(s_xn2, n + 1)
                for s in range(2):
                    last = nc.tensor.transpose(misc[:, s * P:(s + 1) * P], normed[:, s, :], ident[:, :])
                last.then_inc(s_xn2T, 1)

            def router(n):
                for s in range(2):
                    last = mm(misc[:, s * E:(s + 1) * E], xn2T[:, s * P:(s + 1) * P], wr_sb[:, :], start=True, stop=True)
                last.then_inc(s_lg, 1)

            pe.wait_ge(c_pool, 5)
            prep_T(0)
            pe.wait_ge(ld_qkv, 16 * 3)
            query_key(0)
            values(0)
            pe.wait_ge(c_dve, 2)
            pe.wait_ge(ld_mask, 16 * 3 * QUADS)
            pe.wait_ge(ld_w, 16 * 18)
            for k in range(LEAD):
                score(0, k)
            pe.wait_ge(s_v_sb, 1)

            def counts(g):
                pe.wait_ge(s_sel, g + 1)
                sel = r_sel[:, :, :].rearrange("p t e -> p (t e)")
                W = (GROUP + 1) * E
                mm(misc[:, COUNTS:COUNTS + W], before[:, :], sel, start=True, stop=False)
                for back in range(1, GROUP + 1):
                    last = mm(misc[:, COUNTS + back * E:COUNTS + W], ones[:, :], sel[:, 0:W - back * E], start=False, stop=(back == GROUP))
                last.then_inc(s_pos, 1)

            def pair(n, g=None, first=False):
                for k in range(UNITS):
                    probs_T(n, k)
                    if k + LEAD < UNITS:
                        score(n, k + LEAD)
                    else:
                        score(n + 1, k + LEAD - UNITS)
                    if k > 0:
                        weighted(n, k - 1)
                    elif not first:
                        weighted(n - 1, UNITS - 1)
                    if k == 0:
                        pe.wait_ge(s_lg_sb, START + n)
                        prep_T(n + 1)
                    if k == 1:
                        if not first:
                            context_T(n - 1, 1)
                        query_key(n + 1)
                    if k == 2 and not first:
                        project(n - 1, 1)
                    if k == 3:
                        values(n + 1)
                    if k == 5:
                        pe.wait_ge(s_v_sb, n + 2)
                        router_T(n)
                    if k == 6:
                        context_T(n, 0)
                        pe.wait_ge(s_xn2T_sb, n + 1)
                        if g is not None:
                            counts(g)
                        router(n)
                    if k == 7:
                        project(n, 0)

            pair(0, first=True)
            pe.wait_ge(c_pool, 21)
            walk(pe, pair)
            weighted(NPAIR - 1, UNITS - 1)
            context_T(NPAIR - 1, 1)
            project(NPAIR - 1, 1)
            pe.wait_ge(s_lg_sb, START + NPAIR)
            router_T(NPAIR)
            pe.wait_ge(s_xn2T_sb, NPAIR + 1)
            router(NPAIR)
            pe.wait_ge(s_lg_sb, START + NPAIR + 1)
            router_T(NPAIR + 1, last_normed)
            pe.wait_ge(s_xn2T_sb, NPAIR + 2)
            router(NPAIR + 1)
            pe.wait_ge(s_lg_sb, START + NPAIR + 2)
            counts(NGROUP - 1)

            PARTS = ((0, 0), (0, 1), (1, 0))

            def slots_T(ee, c):
                pe.wait_ge(ld_g[c // CHUNKS][c % CHUNKS], 16 * ee + 16)
                for k in range(4):
                    last = nc.tensor.transpose(pt_ps[:, k * P:(k + 1) * P],
                                               xg[:, c // CHUNKS, (c % CHUNKS) * 4 + k, 0:D], ident[:, :])
                last.then_inc(f_xT, 1)

            def hidden(ee, c, first):
                r, q = c // CHUNKS, ee * 2 * CHUNKS + c
                if c % CHUNKS == 0:
                    pe.wait_ge(f_w_hl, 2 * ee + r + 1)
                pe.wait_ge(f_xT_lo, q + 1)
                for f in range(FC):
                    if not (first and c == 0):
                        pe.wait_ge(f_gelu, (q - 1) * FC + f + 1)
                    for i, (a, b) in enumerate(PARTS):
                        last = mm(bank[f][:, :], w1_hl[:, r, a, f * P:(f + 1) * P], xT_hl[:, c % 2, b, :],
                                  start=(i == 0), stop=(i == 2))
                    last.then_inc(f_h, 1)

            def results(q, c):
                r = c // CHUNKS
                pe.wait_ge(f_gelu, q * FC + FC)
                pe.wait_ge(f_y_sb, q + 1)
                for k in range(4):
                    for f in range(FC):
                        last = mm(o_ps[c % 2][:, k * D:(k + 1) * D], hT[:, c % 2, f, k * P:(k + 1) * P],
                                  w2_sb[:, r, f, :], start=(f == 0), stop=(f == FC - 1))
                last.then_inc(f_y, 1)

            def experts(ee, first=False, last=False):
                for c in range(2 * CHUNKS):
                    q = ee * 2 * CHUNKS + c
                    hidden(ee, c, first)
                    if c + 1 < 2 * CHUNKS:
                        slots_T(ee, c + 1)
                    elif not last:
                        slots_T(ee + 1, 0)
                    if c > 0:
                        results(q - 1, c - 1)
                    elif not first:
                        results(q - 1, 2 * CHUNKS - 1)
                if last:
                    results(E * CHUNKS - 1, 2 * CHUNKS - 1)

            pe.wait_ge(s_x2, START + 2 * NPAIR)
            pe.wait_ge(s_max, UNITS * NPAIR + LEAD)
            slots_T(0, 0)
            experts(0, first=True)
            with pe.Fori(1, E // 2 - 1) as ee:
                experts(ee)
            experts(E // 2 - 1, last=True)


_INS = ["L0_attn_x", "L0_attn_Wq", "L0_attn_Wk", "L0_attn_Wv", "L0_attn_Wo", "L0_ffn_w_router",
        "L0_ffn_w1", "L0_ffn_w2", "L0_ffn_bias"]


def kernel(**inputs):
    import numpy as _np
    import concourse.bacc as _bacc
    from concourse import mybir as _mybir
    from concourse.bass_utils import run_bass_kernel_spmd as _run

    nc = _bacc.Bacc("TRN2", target_bir_lowering=False, num_devices=1)
    arrays, args = {}, []
    for name in _INS:
        a = _np.ascontiguousarray(inputs[name])
        arrays[f"in_{name}"] = a
        args.append(nc.dram_tensor(f"in_{name}", a.shape, _mybir.dt.from_np(a.dtype), kind="ExternalInput").ap())
    out = nc.dram_tensor("out_0", (T + CAP, D), _mybir.dt.float32, kind="ExternalOutput").ap()
    moe_block_kernel(nc, *args, out)
    r = _run(nc, [arrays], core_ids=[0])
    return r.results[0]["out_0"][0:T].reshape(BATCH, SEQ, D)
```
